# Optimizing a Trainium2 kernel written in Bass

```python
import numpy as np
import jax
import jax.numpy as jnp

def _softmax(x, axis=-1):
    return jax.nn.softmax(x, axis=axis)

def _gelu(x):
    return jax.nn.gelu(x, approximate=True)

def _silu(x):
    return jax.nn.silu(x)

def _sigmoid(x):
    return jax.nn.sigmoid(x)

def _layernorm(x, axis=-1, eps=1e-05):
    m = jnp.mean(x, axis=axis, keepdims=True)
    v = jnp.var(x, axis=axis, keepdims=True)
    return (x - m) / jnp.sqrt(v + eps)

def _scatter_add(tgt, idx, src, axis=0):
    return tgt.at[idx].add(src)

def _segment_sum(src, seg, n):
    return jax.ops.segment_sum(src, seg, n)
kernel_name = 'mk_vit_tower_d1_tok_img512_r4_8e197e'

def setup_inputs(seed: int=0):
    np.random.seed(seed)
    _w = jnp.asarray

    def _rec_inputs():
        import jax
        import jax.numpy as jnp
        _rk = jax.random.key(seed)
        x = -0.000121822 + 0.999869 * jax.random.normal(jax.random.fold_in(_rk, 1), (128, 3, 196, 196), jnp.float32)
        return x
    x = _rec_inputs()

    def _L0_tok_setup():
        import jax, jax.numpy as jnp
        import numpy as np
        B, C, H, N_P, HID = (64, 3, 196, 14, 128)
        P = H // N_P
        IN_DIM = C * P * P
        SEQ = N_P * N_P + 1

        def sinusoidal_position(length, d):
            pos = jnp.arange(length, dtype=jnp.float32)[:, None]
            i = jnp.arange(d)[None, :]
            angle = pos / jnp.power(10000.0, (2 * (i // 2)).astype(jnp.float32) / d)
            return jnp.where(i % 2 == 0, jnp.sin(angle), jnp.cos(angle)).astype(jnp.float32)
        key = jax.random.key(seed)
        k_img, k_w, k_b, k_tok = jax.random.split(key, 4)
        img = jax.random.normal(k_img, (B, C, H, H), dtype=jnp.float32)
        W = jax.random.normal(k_w, (HID, IN_DIM), dtype=jnp.float32) / np.sqrt(IN_DIM)
        b = jax.random.normal(k_b, (HID,), dtype=jnp.float32) * 0.01
        token = jax.random.uniform(k_tok, (1, HID), dtype=jnp.float32)
        pos = sinusoidal_position(SEQ, HID)
        return {'img': img, 'W': W, 'b': b, 'token': token, 'pos': pos}
    _L0_tok_all = _L0_tok_setup()
    _L0_tok_in = {k: v for k, v in _L0_tok_all.items() if k in ('W', 'b', 'token', 'pos')}
    del _L0_tok_all

    def _L0_attn_setup():
        import jax, jax.numpy as jnp
        import numpy as np
        D_MODEL = 128
        HEADS = 8
        D_K = D_MODEL // HEADS
        BATCH, N = (4, 512)
        key = jax.random.key(seed)
        ks = jax.random.split(key, 6)
        xavier = (6.0 / (D_K + D_MODEL)) ** 0.5
        latent = jax.random.normal(ks[0], (BATCH, N, D_MODEL), dtype=jnp.float32)
        q_proj = jax.random.uniform(ks[1], (HEADS, D_MODEL, D_K), minval=-xavier, maxval=xavier, dtype=jnp.float32)
        k_proj = jax.random.uniform(ks[2], (HEADS, D_MODEL, D_K), minval=-xavier, maxval=xavier, dtype=jnp.float32)
        v_proj = jax.random.uniform(ks[3], (HEADS, D_MODEL, D_K), minval=-xavier, maxval=xavier, dtype=jnp.float32)
        q_bias = jnp.zeros((HEADS, D_K), dtype=jnp.float32)
        k_bias = jnp.zeros((HEADS, D_K), dtype=jnp.float32)
        v_bias = jnp.zeros((HEADS, D_K), dtype=jnp.float32)
        out_w = jax.random.normal(ks[4], (D_MODEL, D_MODEL), dtype=jnp.float32) * (1.0 / D_MODEL ** 0.5)
        return {'latent': latent, 'q_proj': q_proj, 'k_proj': k_proj, 'v_proj': v_proj, 'q_bias': q_bias, 'k_bias': k_bias, 'v_bias': v_bias, 'out_w': out_w}
    _L0_attn_all = _L0_attn_setup()
    _L0_attn_in = {k: v for k, v in _L0_attn_all.items() if k in ('q_proj', 'k_proj', 'v_proj', 'q_bias', 'k_bias', 'v_bias', 'out_w')}
    del _L0_attn_all

    def _L0_ffn_setup():
        import jax, jax.numpy as jnp
        import numpy as np
        T = 128
        B = 64
        C = 256

        def _triu_apply(x, W, b):
            Wm = jnp.tril(W)
            return jnp.einsum('bct,st->bcs', x, Wm) + b
        key = jax.random.key(seed)
        ks = jax.random.split(key, 5)
        x = jax.random.normal(ks[0], (B, C, T), dtype=jnp.float32)
        scale = 1.0 / jnp.sqrt(jnp.arange(1, T + 1, dtype=jnp.float32))[:, None]
        W1 = jax.random.uniform(ks[1], (T, T), jnp.float32, -1.0, 1.0) * scale
        b1 = jax.random.uniform(ks[2], (T,), jnp.float32, -1.0, 1.0) * scale[:, 0]
        W2 = jax.random.uniform(ks[3], (T, T), jnp.float32, -1.0, 1.0) * scale
        b2 = jax.random.uniform(ks[4], (T,), jnp.float32, -1.0, 1.0) * scale[:, 0]
        return {'x': x, 'W1': W1, 'b1': b1, 'W2': W2, 'b2': b2}
    _L0_ffn_all = _L0_ffn_setup()
    _L0_ffn_in = {k: v for k, v in _L0_ffn_all.items() if k in ('W1', 'b1', 'W2', 'b2')}
    del _L0_ffn_all
    return {'x': x, 'L0_tok_W': _L0_tok_in['W'], 'L0_tok_b': _L0_tok_in['b'], 'L0_tok_token': _L0_tok_in['token'], 'L0_tok_pos': _L0_tok_in['pos'], 'L0_attn_q_proj': _L0_attn_in['q_proj'], 'L0_attn_k_proj': _L0_attn_in['k_proj'], 'L0_attn_v_proj': _L0_attn_in['v_proj'], 'L0_attn_q_bias': _L0_attn_in['q_bias'], 'L0_attn_k_bias': _L0_attn_in['k_bias'], 'L0_attn_v_bias': _L0_attn_in['v_bias'], 'L0_attn_out_w': _L0_attn_in['out_w'], 'L0_ffn_W1': _L0_ffn_in['W1'], 'L0_ffn_b1': _L0_ffn_in['b1'], 'L0_ffn_W2': _L0_ffn_in['W2'], 'L0_ffn_b2': _L0_ffn_in['b2']}

def reference(x, L0_tok_W, L0_tok_b, L0_tok_token, L0_tok_pos, L0_attn_q_proj, L0_attn_k_proj, L0_attn_v_proj, L0_attn_q_bias, L0_attn_k_bias, L0_attn_v_bias, L0_attn_out_w, L0_ffn_W1, L0_ffn_b1, L0_ffn_W2, L0_ffn_b2):
    import jax
    import jax.numpy as jnp

    def _L0_tok_ref(img, W, b, token, pos):
        import jax, jax.numpy as jnp
        import numpy as np
        B, C, H, N_P, HID = (64, 3, 196, 14, 128)
        P = H // N_P
        IN_DIM = C * P * P
        SEQ = N_P * N_P + 1

        def sinusoidal_position(length, d):
            pos = jnp.arange(length, dtype=jnp.float32)[:, None]
            i = jnp.arange(d)[None, :]
            angle = pos / jnp.power(10000.0, (2 * (i // 2)).astype(jnp.float32) / d)
            return jnp.where(i % 2 == 0, jnp.sin(angle), jnp.cos(angle)).astype(jnp.float32)
        Bn = img.shape[0]
        patches = img.reshape(Bn, C, N_P, P, N_P, P)
        patches = patches.transpose(0, 2, 4, 1, 3, 5).reshape(Bn, N_P * N_P, IN_DIM)
        tokens = jnp.einsum('bsd,hd->bsh', patches, W) + b
        cls = jnp.broadcast_to(token[None, :, :], (Bn, 1, HID))
        out = jnp.concatenate([cls, tokens], axis=1) + pos
        return out

    def _L0_attn_ref(latent, q_proj, k_proj, v_proj, q_bias, k_bias, v_bias, out_w):
        import jax, jax.numpy as jnp
        import numpy as np
        D_MODEL = 128
        HEADS = 8
        D_K = D_MODEL // HEADS
        BATCH, N = (4, 512)
        b, n, d = latent.shape
        Q = jnp.einsum('bnd,hdk->bhnk', latent, q_proj) + q_bias[None, :, None, :]
        K = jnp.einsum('bnd,hdk->bhnk', latent, k_proj) + k_bias[None, :, None, :]
        V = jnp.einsum('bnd,hdk->bhnk', latent, v_proj) + v_bias[None, :, None, :]
        S = jnp.einsum('bhqk,bhmk->bhqm', Q, K) / D_K ** 0.5
        P = jax.nn.softmax(S, axis=-1)
        out = jnp.einsum('bhqm,bhmk->bhqk', P, V)
        out = jnp.transpose(out, (0, 2, 3, 1)).reshape(b, n, d)
        return out @ out_w.T

    def _L0_ffn_ref(x, W1, b1, W2, b2):
        import jax, jax.numpy as jnp
        import numpy as np
        T = 128
        B = 64
        C = 256

        def _triu_apply(x, W, b):
            Wm = jnp.tril(W)
            return jnp.einsum('bct,st->bcs', x, Wm) + b
        h = _triu_apply(x, W1, b1)
        h = jax.nn.gelu(h, approximate=False)
        return _triu_apply(h, W2, b2)
    h = _L0_tok_ref(x, L0_tok_W, L0_tok_b, L0_tok_token, L0_tok_pos)
    h = h + _L0_attn_ref(_layernorm(h, axis=-1), L0_attn_q_proj, L0_attn_k_proj, L0_attn_v_proj, L0_attn_q_bias, L0_attn_k_bias, L0_attn_v_bias, L0_attn_out_w)
    h = h + _L0_ffn_ref(_layernorm(h, axis=-1), L0_ffn_W1, L0_ffn_b1, L0_ffn_W2, L0_ffn_b2)
    return h

_drawn_inputs = setup_inputs


def setup_inputs(seed=0):
    import zlib

    import numpy as np

    out = dict(_drawn_inputs(seed))
    spreads = {'L0_attn_q_bias': (0.0, 0.28), 'L0_attn_k_bias': (0.0, 0.8), 'L0_attn_v_bias': (0.0, 0.1)}
    factors = {'L0_tok_b': 4.79}
    for name, (base, spread) in spreads.items():
        noise = np.random.default_rng([zlib.crc32(name.encode()), seed]).standard_normal(out[name].shape)
        drawn = base * np.exp(spread * noise) if base else spread * noise
        out[name] = jnp.asarray(drawn.astype(out[name].dtype))
    for name, factor in factors.items():
        out[name] = (out[name] * factor).astype(out[name].dtype)
    return out
```

```python
import concourse.bass as bass
from concourse import mybir
from contextlib import ExitStack

F32 = mybir.dt.float32
F32R = mybir.dt.float32r
ALU = mybir.AluOpType
ACT = mybir.ActivationFunctionType
AX = mybir.AxisListType

B, C, IMG, GRID, D, H, DK = 128, 3, 196, 14, 128, 8, 16
PATCH = IMG // GRID
NPATCH = GRID * GRID
SEQ = NPATCH + 1
W = SEQ + 1
PAIRS = B // 2
SHIFTS = 3
ROWS = C * PATCH
STEPS = -(-PATCH // SHIFTS)
XW = 2 * GRID * IMG
TILE = ((0, 100), (100, 98))
KEYS = (100, 97)
G = 2
Q4 = 4
EPS = 1e-5


def vit_kernel(nc, x, wtok, wq, wk, wv, wo, w1, w2, tril_mask, center, mean, ident, pos2, cls_tok, cls_pos,
               cols, vbias, b2, out):
    ctx = ExitStack()
    with ctx:
        def sb(name, shape, dt=F32):
            return ctx.enter_context(nc.sbuf_tensor(name, shape, dt))

        def sem(name):
            return ctx.enter_context(nc.semaphore(name))

        wtok_sb = sb("wtok_sb", [SHIFTS * ROWS, STEPS, D])
        wq_sb = sb("wq_sb", [D, G, 128])
        wk_sb = sb("wk_sb", [D, G, 128])
        wv_sb = sb("wv_sb", [D, D])
        wo_sb = sb("wo_sb", [128, G, D])
        w1_raw = sb("w1_raw", [D, D])
        w2_raw = sb("w2_raw", [D, D])
        w1_sb = sb("w1_sb", [D, D])
        w2_sb = sb("w2_sb", [D, D])
        tril_sb = sb("tril_sb", [D, D])
        center_sb = sb("center_sb", [D, D])
        mean_sb = sb("mean_sb", [D, D])
        ident_sb = sb("ident_sb", [D, D])
        neg_ident = sb("neg_ident", [D, 100], F32R)
        pos_raw = sb("pos_raw", [D, 2, NPATCH])
        pos_b = sb("pos_b", [D, 2, NPATCH])
        cls_raw = sb("cls_raw", [D, 2])
        cols_sb = sb("cols_sb", [D, 10])
        vb_sb = sb("vb_sb", [100, 2 * D])
        b2_sb = sb("b2_sb", [100, 4 * D])
        tok_b, b1_c = cols_sb[:, 0:1], cols_sb[:, 1:2]
        eps_c = cols_sb[:, 9:10]
        mask_lo, mask_hi, one_16 = cols_sb[:, 2:3], cols_sb[:, 3:4], cols_sb[:, 4:5]
        qb = [cols_sb[:, 5 + g:6 + g] for g in range(G)]
        kb = [cols_sb[:, 7 + g:8 + g] for g in range(G)]
        qb_hi = sb("qb_hi", [D, G])

        pixels = [sb(f"pixels{p}", [SHIFTS * ROWS, XW]) for p in range(2)]
        h = [sb(f"h{p}", [D, 2, W]) for p in range(2)]
        sq1, std1, rstd1, xhat1 = [sb(name, [D, 2 * W]) for name in ("sq1", "std1", "rstd1", "xhat1")]
        sq2, std2, rstd2, xhat2 = [sb(name, [D, 2 * W]) for name in ("sq2", "std2", "rstd2", "xhat2")]
        q_sub = sb("q_sub", [128, G, 2, W], F32R)
        q_hl = [sb(f"q_hl{p}", [128, 2, G, W], F32R) for p in range(2)]
        k_hi = [sb(f"k_hi{p}", [128, 2, G, W], F32R) for p in range(2)]
        k_raw = sb("k_raw", [128, G, 2, W])
        k_lo = [sb(f"k_lo{p}", [128, 2, G, W], F32R) for p in range(2)]
        q_max = [sb(f"q_max{m}", [128, G * W], F32R) for m in range(2)]
        v = [sb(f"v{p}", [100, 2, 2, H, 32]) for p in range(2)]
        row_max = [sb(f"row_max{m}", [100, 2, G, 128], F32R) for m in range(2)]
        probs = [sb(f"probs{m}", [100, 2, Q4, G * W]) for m in range(2)]
        recip = sb("recip", [128, G * W])
        inv_den = sb("inv_den", [128, G * W])
        attn = sb("attn", [128, 2, G, W])
        pool_tick, dve_tick = sb("pool_tick", [128, 2]), sb("dve_tick", [128, 2])
        h2 = sb("h2", [D, 2, W])
        gelu = sb("gelu", [D, 2, W])
        out_sb = [sb(f"out_sb{p}", [100, 2, 2, D]) for p in range(2)]

        bank = [ctx.enter_context(nc.psum_tensor(f"bank{n}", [128, 512], F32)) for n in range(8)]
        M0, M1, M2, M3 = bank[0:4]
        SA, ST = bank[4:6], bank[6:8]

        const_in = sem("const_in")
        pixels_in = [sem(f"pixels_in{p}") for p in range(2)]
        shifts_in = [sem(f"shifts_in{p}") for p in range(2)]
        stored = [sem(f"stored{p}") for p in range(2)]
        setup, pool_setup = sem("setup"), sem("pool_setup")
        tok_done, xc1_done, var1_done = sem("tok_done"), sem("xc1_done"), sem("var1_done")
        q_done, k_done, v_done = sem("q_done"), sem("k_done"), sem("v_done")
        score_done = sem("score_done")
        score_t_done = sem("score_t_done")
        max_t_done, pv_done = sem("max_t_done"), sem("pv_done")
        oproj_done, xc2_done, var2_done = sem("oproj_done"), sem("xc2_done"), sem("var2_done")
        ffn1_done, ffn2_done = sem("ffn1_done"), sem("ffn2_done")
        h_ready, rstd1_ready, xhat1_ready = sem("h_ready"), sem("rstd1_ready"), sem("xhat1_ready")
        q_hl_ready, k_raw_ready, v_ready = sem("q_hl_ready"), sem("k_raw_ready"), sem("v_ready")
        max_ready = sem("max_ready")
        q_max_ready, attn_ready = sem("q_max_ready"), sem("attn_ready")
        recip_ready, inv_den_ready = sem("recip_ready"), sem("inv_den_ready")
        h2_ready, rstd2_ready, xhat2_ready = sem("h2_ready"), sem("rstd2_ready"), sem("xhat2_ready")
        out_ready = sem("out_ready")
        std1_ready, std2_ready = sem("std1_ready"), sem("std2_ready")
        sq1_ready, sq2_ready, gelu_ready = sem("sq1_ready"), sem("sq2_ready"), sem("gelu_ready")
        q_sub_ready, k_hi_ready = sem("q_sub_ready"), sem("k_hi_ready")
        exp_ready = sem("exp_ready")
        k_lo_ready = sem("k_lo_ready")

        def upto(eng, s, count):
            if not isinstance(count, int) or count > 0:
                eng.wait_ge(s, count)

        def exists(n):
            return not isinstance(n, int) or 0 <= n < PAIRS

        def over_pairs(eng, body, last):
            body(0, 0, 0)
            loops = last // 2
            with eng.Fori(0, loops) as k:
                body(2 * k + 1, k, 1)
                body(2 * k + 2, k + 1, 0)
            for n in range(2 * loops + 1, last + 1):
                body(n, n // 2, n % 2)

        consts = [(wtok_sb, wtok), (wq_sb, wq), (wk_sb, wk), (wv_sb, wv), (wo_sb, wo), (w1_raw, w1), (w2_raw, w2),
                  (tril_sb, tril_mask), (center_sb, center), (mean_sb, mean), (ident_sb, ident),
                  (pos_raw, pos2), (cols_sb, cols), (vb_sb, vbias), (b2_sb, b2)]
        CONSTS = 16 * (len(consts) + 2)
        SETUP = 13

        block = ctx.enter_context(nc.Block())

        @block.sync
        def _(sp):
            def load_pixels(n, half, par):
                if not isinstance(n, int) or n >= 2:
                    sp.wait_ge(tok_done, n - 1)
                for m in range(2):
                    for c in range(C):
                        sp.dma_start(
                            pixels[par][PATCH * c:PATCH * (c + 1), m * XW // 2:(m + 1) * XW // 2],
                            x[bass.ds(2 * n + m, 1), c, :, :].rearrange("m (i p) w -> p (m i) w", p=PATCH),
                        ).then_inc(pixels_in[par], 16)
                sp.wait_ge(pixels_in[par], 96 * (half + 1))
                for s in range(1, SHIFTS):
                    sp.dma_start(pixels[par][ROWS * s:ROWS * (s + 1), 0:XW - s],
                                 pixels[par][0:ROWS, s:XW]).then_inc(shifts_in[par], 16)

            def store(n, half, par):
                sp.wait_ge(out_ready, n + 1)
                tokens = out[bass.ds(2 * n, 2), :, :].rearrange("m t d -> t m d")
                for t0, rows, src in ((0, 100, out_sb[par][0:100, :, 0, :]),
                                      (100, 96, out_sb[par][0:96, :, 1, :]),
                                      (196, 1, out_sb[par][96:97, :, 1, :])):
                    sp.dma_start(tokens[t0:t0 + rows, :, :], src).then_inc(stored[par], 16)

            load_pixels(0, 0, 0)
            for dst, src in consts:
                sp.dma_start(dst[:], src).then_inc(const_in, 16)
            sp.dma_start(cls_raw[:, 0:1], cls_tok).then_inc(const_in, 16)
            sp.dma_start(cls_raw[:, 1:2], cls_pos).then_inc(const_in, 16)
            load_pixels(1, 0, 1)
            load_pixels(2, 1, 0)
            with sp.Fori(0, (PAIRS - 4) // 2) as k:
                load_pixels(2 * k + 3, k + 1, 1)
                store(2 * k, k, 0)
                load_pixels(2 * k + 4, k + 2, 0)
                store(2 * k + 1, k, 1)
            load_pixels(PAIRS - 1, (PAIRS - 1) // 2, 1)
            for n in range(PAIRS - 4, PAIRS):
                store(n, n // 2, n % 2)
            for p in range(2):
                sp.wait_ge(stored[p], 48 * PAIRS // 2)

        @block.gpsimd
        def _(pool):
            def make_k_lo(n, half, par):
                for g in range(G):
                    pool.wait_ge(k_raw_ready, 2 * n + g + 1)
                    upto(pool, k_lo_ready, 2 * n + g)
                    nc.gpsimd.tensor_tensor(pool_tick[:, 1:2], pool_tick[:, 0:1], pool_tick[:, 0:1], ALU.add)
                    nc.gpsimd.tensor_scalar(k_lo[par][:, :, g, :], k_raw[:, g, :, :], mask_lo, one_16,
                                            ALU.mult, ALU.add).then_inc(k_lo_ready, 1)
            pool.wait_ge(const_in, CONSTS)
            nc.gpsimd.memset(pool_tick[:, :], 0.0).then_inc(pool_setup, 1)
            pool.wait_ge(pool_setup, 1)
            over_pairs(pool, make_k_lo, PAIRS - 1)

        @block.scalar
        def _(act):
            def square(xc_done, bank_, sq, ready, n):
                act.wait_ge(xc_done, n + 1)
                nc.scalar.activation(sq[:, :], bank_[:, 0:2 * W], ACT.Square).then_inc(ready, 1)

            def deviation(var_done, bank_, std, ready, n):
                act.wait_ge(var_done, n + 1)
                nc.scalar.activation(std[:, :], bank_[:, 0:2 * W], ACT.Sqrt, bias=eps_c).then_inc(ready, 1)

            def q_high(n, g):
                act.wait_ge(q_done, 2 * n + g + 1)
                upto(act, q_hl_ready, 2 * n + g - 1)
                nc.scalar.activation(q_sub[:, g, :, :], (M3, M0)[g][:, 0:2 * W], ACT.Identity,
                                     bias=qb_hi[:, g:g + 1], scale=mask_hi).then_inc(q_sub_ready, 1)

            def k_high(n, par, g):
                act.wait_ge(k_done, 2 * n + g + 1)
                nc.scalar.activation(k_hi[par][:, :, g, :], (M1, M2)[g][:, 0:2 * W], ACT.Identity,
                                     bias=kb[g]).then_inc(k_hi_ready, 1)

            def exp(n, m, u):
                unit = 16 * n + 8 * m + u
                kt, j = divmod(u, Q4)
                act.wait_ge(score_t_done, unit + 1)
                nc.scalar.activation(probs[m][0:KEYS[kt], kt, j, :], ST[u % 2][0:KEYS[kt], 0:G * W], ACT.Exp,
                                     scale=DK ** -0.5).then_inc(exp_ready, 1)

            def ffn_gelu(n):
                act.wait_ge(ffn1_done, n + 1)
                nc.scalar.activation(gelu[:, :, :], M2[:, 0:2 * W], ACT.Gelu, bias=b1_c).then_inc(gelu_ready, 1)

            def pair(n, half, par):
                prev, nxt = exists(n - 1), exists(n + 1)
                if prev:
                    for u in range(8):
                        exp(n - 1, 1, u)
                for u in range(8):
                    exp(n, 0, u)
                    if u == 1 and nxt:
                        square(xc1_done, M1, sq1, sq1_ready, n + 1)
                    if u == 2 and prev:
                        square(xc2_done, M0, sq2, sq2_ready, n - 1)
                    if u == 4 and nxt:
                        deviation(var1_done, M2, std1, std1_ready, n + 1)
                    if u == 4 and prev:
                        deviation(var2_done, M3, std2, std2_ready, n - 1)
                    if u == 5 and nxt:
                        q_high(n + 1, 0)
                    if u == 6 and nxt:
                        q_high(n + 1, 1)
                if prev:
                    ffn_gelu(n - 1)
                if nxt:
                    for g in range(G):
                        k_high(n + 1, 1 - par, g)

            act.wait_ge(setup, SETUP)
            square(xc1_done, M1, sq1, sq1_ready, 0)
            deviation(var1_done, M2, std1, std1_ready, 0)
            for g in range(G):
                q_high(0, g)
            for g in range(G):
                k_high(0, 0, g)
            over_pairs(act, pair, PAIRS - 1)
            for u in range(8):
                exp(PAIRS - 1, 1, u)
            square(xc2_done, M0, sq2, sq2_ready, PAIRS - 1)
            deviation(var2_done, M3, std2, std2_ready, PAIRS - 1)
            ffn_gelu(PAIRS - 1)

        @block.vector
        def _(dve):
            def embed(n, par):
                dve.wait_ge(tok_done, n + 1)
                upto(dve, h2_ready, n - 1)
                nc.vector.tensor_tensor(h[par][:, :, 1:SEQ], M0[:, 0:2 * NPATCH].rearrange("p (m t) -> p m t", m=2),
                                        pos_b[:, :, :], ALU.add).then_inc(h_ready, 1)

            def normalise(std_ready, std, rstd, rstd_ready, xc_bank, xhat, xhat_ready, n):
                dve.wait_ge(std_ready, n + 1)
                upto(dve, xhat_ready, n)
                nc.vector.reciprocal(rstd[:, :], std[:, :]).then_inc(rstd_ready, 1)
                dve.wait_ge(rstd_ready, n + 1)
                nc.vector.tensor_tensor(xhat[:, :], xc_bank[:, 0:2 * W], rstd[:, :], ALU.mult).then_inc(xhat_ready, 1)

            def norm1(n):
                upto(dve, v_done, n)
                normalise(std1_ready, std1, rstd1, rstd1_ready, M1, xhat1, xhat1_ready, n)

            def norm2(n):
                normalise(std2_ready, std2, rstd2, rstd2_ready, M0, xhat2, xhat2_ready, n)

            def q_split(n, par, g):
                dve.wait_ge(q_sub_ready, 2 * n + g + 1)
                upto(dve, q_max_ready, 2 * n - 2)
                nc.vector.scalar_tensor_tensor(
                    out=q_hl[par][:, :, g, :], in0=(M3, M0)[g][:, 0:2 * W].rearrange("p (m t) -> p m t", m=2),
                    scalar=qb[g], in1=q_sub[:, g, :, :].bitcast(F32), op0=ALU.add, op1=ALU.subtract)\
                    .then_inc(q_hl_ready, 1)

            def k_split(n, par, g):
                dve.wait_ge(k_hi_ready, 2 * n + g + 1)
                upto(dve, k_lo_ready, 2 * n + g - 1)
                nc.vector.scalar_tensor_tensor(
                    out=k_raw[:, g, :, :], in0=(M1, M2)[g][:, 0:2 * W].rearrange("p (m t) -> p m t", m=2),
                    scalar=kb[g], in1=k_hi[par][:, :, g, :].bitcast(F32), op0=ALU.add, op1=ALU.subtract)\
                    .then_inc(k_raw_ready, 1)

            def v_out(n, par):
                dve.wait_ge(v_done, n + 1)
                for kt, rows in enumerate((100, 98)):
                    last = nc.vector.tensor_tensor(
                        v[par][0:rows, :, kt, :, 0:DK],
                        M0[0:rows, :].rearrange("p (m k h d) -> p m k h d", m=2, k=2, h=H)[:, :, kt, :, :],
                        vb_sb[0:rows, :].rearrange("p (m h d) -> p m h d", m=2, h=H), ALU.add)
                last.then_inc(v_ready, 1)

            def maximum(n, m, u):
                unit = 16 * n + 8 * m + u
                qt, j = divmod(u, Q4)
                rows = TILE[qt][1]
                dve.wait_ge(score_done, unit + 1)
                if u == 0:
                    upto(dve, max_t_done, 2 * n + m - 1)
                nc.vector.reduce_max(row_max[m][0:rows, qt, :, 32 * j + DK:32 * j + DK + 1],
                                     SA[u % 2][0:rows, 0:G * W].rearrange("p (g t) -> p g t", g=G)[:, :, 0:SEQ],
                                     AX.X).then_inc(max_ready, 1)

            def add_max(n, par, m):
                dve.wait_ge(max_t_done, 2 * n + m + 1)
                nc.vector.scalar_tensor_tensor(
                    out=q_max[m][:, :], in0=q_hl[par][:, m, :, :].rearrange("p g t -> p (g t)").bitcast(F32),
                    scalar=mask_lo, in1=(M1, M2)[m][:, 0:G * W], op0=ALU.mult, op1=ALU.add).then_inc(q_max_ready, 1)

            def divide(n, m):
                o = (M1, M3)[m]
                dve.wait_ge(pv_done, 2 * n + m + 1)
                upto(dve, attn_ready, 2 * n + m)
                nc.vector.reciprocal(recip[:, :], o[:, 0:G * W]).then_inc(recip_ready, 1)
                dve.wait_ge(recip_ready, 2 * n + m + 1)
                upto(dve, inv_den_ready, 2 * n + m)
                nc.vector.tensor_copy(dve_tick[:, 1:2], dve_tick[:, 0:1])
                nc.vector.stream_shuffle(inv_den[:, :], recip[:, :], [DK] * 32).then_inc(inv_den_ready, 1)
                dve.wait_ge(inv_den_ready, 2 * n + m + 1)
                nc.vector.tensor_tensor(attn[:, m, :, :].rearrange("p g t -> p (g t)"), o[:, 0:G * W], inv_den[:, :],
                                        ALU.mult).then_inc(attn_ready, 1)

            def residual(n, par):
                dve.wait_ge(oproj_done, n + 1)
                nc.vector.tensor_tensor(h2[:, :, :], M2[:, 0:2 * W].rearrange("p (m t) -> p m t", m=2), h[par][:, :, :],
                                        ALU.add).then_inc(h2_ready, 1)

            def output(n, half, par):
                dve.wait_ge(ffn2_done, n + 1)
                upto(dve, stored[par], 48 * half)
                for tt, rows in enumerate((100, 97)):
                    last = nc.vector.tensor_tensor(
                        out_sb[par][0:rows, :, tt, :],
                        M3[0:rows, :].rearrange("p (m t d) -> p m t d", m=2, t=2)[:, :, tt, :],
                        b2_sb[0:rows, 0:2 * D].rearrange("p (m d) -> p m d", m=2), ALU.add)
                last.then_inc(out_ready, 1)

            def pair(n, half, par):
                prev, nxt = exists(n - 1), exists(n + 1)
                for u in range(8):
                    maximum(n, 0, u)
                if prev:
                    divide(n - 1, 1)
                add_max(n, par, 0)
                maximum(n, 1, 0)
                if prev:
                    residual(n - 1, 1 - par)
                maximum(n, 1, 1)
                if nxt:
                    embed(n + 1, 1 - par)
                maximum(n, 1, 2)
                maximum(n, 1, 3)
                maximum(n, 1, 4)
                if nxt:
                    norm1(n + 1)
                if prev:
                    norm2(n - 1)
                maximum(n, 1, 5)
                if nxt:
                    q_split(n + 1, 1 - par, 0)
                maximum(n, 1, 6)
                if nxt:
                    q_split(n + 1, 1 - par, 1)
                maximum(n, 1, 7)
                if nxt:
                    k_split(n + 1, 1 - par, 0)
                    k_split(n + 1, 1 - par, 1)
                    v_out(n + 1, 1 - par)
                divide(n, 0)
                if prev:
                    output(n - 1, half if par == 1 else half - 1, 1 - par)
                add_max(n, par, 1)

            nc.vector.memset(dve_tick[:, :], 0.0).then_inc(setup, 1)
            dve.wait_ge(const_in, CONSTS)
            nc.vector.tensor_tensor(w1_sb[:, :], w1_raw[:, :], tril_sb[:, :], ALU.mult).then_inc(setup, 1)
            nc.vector.tensor_tensor(w2_sb[:, :], w2_raw[:, :], tril_sb[:, :], ALU.mult).then_inc(setup, 1)
            nc.vector.tensor_scalar(neg_ident[:, :], ident_sb[:, 0:100], -1.0, None, ALU.mult).then_inc(setup, 1)
            nc.vector.tensor_scalar(pos_b[:, :, :], pos_raw[:, :, :], tok_b, None, ALU.add).then_inc(setup, 1)
            nc.vector.tensor_scalar(qb_hi[:, :], cols_sb[:, 5:7], mask_hi, None, ALU.mult).then_inc(setup, 1)
            for p in range(2):
                nc.vector.memset(h[p][:, :, W - 1:W], 0.0)
                for m in range(2):
                    last = nc.vector.tensor_tensor(h[p][:, m, 0:1], cls_raw[:, 0:1], cls_raw[:, 1:2], ALU.add)
                last.then_inc(setup, 1)
                nc.vector.memset(v[p][:, :, :, :, DK:32], 1.0).then_inc(setup, 1)
            for m in range(2):
                nc.vector.memset(row_max[m][:, :, :, :].bitcast(F32), 0.0).then_inc(setup, 1)
            nc.vector.memset(attn[:, :, :, :], 0.0).then_inc(setup, 1)
            dve.wait_ge(setup, SETUP)
            embed(0, 0)
            norm1(0)
            for g in range(G):
                q_split(0, 0, g)
            for g in range(G):
                k_split(0, 0, g)
            v_out(0, 0)
            over_pairs(dve, pair, PAIRS - 1)
            n = PAIRS - 1
            divide(n, 1)
            residual(n, n % 2)
            norm2(n)
            output(n, n // 2, n % 2)

        @block.tensor
        def _(pe):
            mm = nc.tensor.matmul

            def embed(n, half, par, t):
                rows = min(SHIFTS, PATCH - SHIFTS * t) * ROWS
                if t == 0:
                    pe.wait_ge(shifts_in[par], 32 * (half + 1))
                    upto(pe, v_ready, n)
                view = pixels[par][:, :].rearrange("p (r j q) -> p r j q", j=GRID, q=PATCH)
                last = mm(M0[:, 0:2 * NPATCH], wtok_sb[0:rows, t, :], view[0:rows, :, :, SHIFTS * t],
                          start=t == 0, stop=t == STEPS - 1)
                if t == STEPS - 1:
                    last.then_inc(tok_done, 1)

            def centre1(n, par):
                pe.wait_ge(h_ready, n + 1)
                upto(pe, q_max_ready, 2 * n - 1)
                mm(M1[:, 0:2 * W], center_sb[:, :], h[par][:, :, :], start=True, stop=True).then_inc(xc1_done, 1)

            def variance1(n):
                pe.wait_ge(sq1_ready, n + 1)
                upto(pe, h2_ready, n - 1)
                mm(M2[:, 0:2 * W], mean_sb[:, :], sq1[:, :], start=True, stop=True).then_inc(var1_done, 1)

            def project_q(n, g):
                pe.wait_ge(xhat1_ready, n + 1)
                if g == 0:
                    upto(pe, std2_ready, n - 1)
                else:
                    upto(pe, xhat2_ready, n - 1)
                mm((M3, M0)[g][:, 0:2 * W], wq_sb[:, g, :], xhat1[:, :], start=True, stop=True).then_inc(q_done, 1)

            def project_k(n, g):
                if g == 1:
                    upto(pe, gelu_ready, n - 1)
                mm((M1, M2)[g][:, 0:2 * W], wk_sb[:, g, :], xhat1[:, :], start=True, stop=True).then_inc(k_done, 1)

            def project_v(n):
                pe.wait_ge(q_hl_ready, 2 * n + 2)
                for m in range(2):
                    for kt, (t0, rows) in enumerate(TILE):
                        c = (2 * m + kt) * D
                        last = mm(M0[0:rows, c:c + D], xhat1[:, m * W + t0:m * W + t0 + rows], wv_sb[:, :],
                                  start=True, stop=True)
                last.then_inc(v_done, 1)

            def scores(n, par, m, u):
                unit = 16 * n + 8 * m + u
                qt, j = divmod(u, Q4)
                t0, rows = TILE[qt]
                r = slice(32 * j, 32 * j + 32)
                if m == 0 and u == 0:
                    pe.wait_ge(q_hl_ready, 2 * n + 2)
                    pe.wait_ge(k_hi_ready, 2 * n + 2)
                upto(pe, max_ready, unit - 1)
                for g in range(G):
                    last = mm(SA[u % 2][0:rows, g * W:(g + 1) * W], q_hl[par][r, m, g, t0:t0 + rows],
                              k_hi[par][r, m, g, :], start=True, stop=True)
                last.then_inc(score_done, 1)

            def transpose_max(n, m):
                pe.wait_ge(max_ready, 16 * n + 8 * m + 8)
                if m == 0:
                    upto(pe, attn_ready, 2 * n - 1)
                elif exists(n + 1):
                    pe.wait_ge(k_raw_ready, 2 * n + 4)
                for qt, (t0, rows) in enumerate(TILE):
                    for g in range(G):
                        last = mm((M1, M2)[m][:, g * W + t0:g * W + t0 + rows], row_max[m][0:rows, qt, g, :],
                                  neg_ident[0:rows, 0:rows], start=True, stop=True)
                last.then_inc(max_t_done, 1)

            def scores_t(n, par, m, u):
                unit = 16 * n + 8 * m + u
                kt, j = divmod(u, Q4)
                t0, rows = TILE[kt][0], KEYS[kt]
                r = slice(32 * j, 32 * j + 32)
                if u == 0:
                    pe.wait_ge(k_lo_ready, 2 * n + 2)
                    pe.wait_ge(q_max_ready, 2 * n + m + 1)
                upto(pe, exp_ready, unit - 1)
                for g in range(G):
                    cols_ = slice(g * W, (g + 1) * W)
                    mm(ST[u % 2][0:rows, cols_], k_hi[par][r, m, g, t0:t0 + rows], q_hl[par][r, m, g, :],
                       start=True, stop=False)
                    last = mm(ST[u % 2][0:rows, cols_], k_lo[par][r, m, g, t0:t0 + rows], q_max[m][r, cols_],
                              start=False, stop=True)
                last.then_inc(score_t_done, 1)

            def weigh_v(n, par, m):
                pe.wait_ge(exp_ready, 16 * n + 8 * m + 8)
                pe.wait_ge(v_ready, n + 1)
                if m == 0:
                    if exists(n + 1):
                        pe.wait_ge(k_raw_ready, 2 * n + 3)
                else:
                    upto(pe, out_ready, n)
                for g in range(G):
                    for kt in range(2):
                        for j in range(Q4):
                            last = mm((M1, M3)[m][32 * j:32 * j + 32, g * W:(g + 1) * W],
                                      v[par][0:KEYS[kt], m, kt, 4 * g + j, :],
                                      probs[m][0:KEYS[kt], kt, j, g * W:(g + 1) * W],
                                      start=kt == 0, stop=kt == 1)
                last.then_inc(pv_done, 1)

            def project_out(n):
                pe.wait_ge(attn_ready, 2 * n + 2)
                upto(pe, q_max_ready, 2 * n + 2)
                for g in range(G):
                    last = mm(M2[:, 0:2 * W], wo_sb[:, g, :], attn[:, :, g, :], start=g == 0, stop=g == 1)
                last.then_inc(oproj_done, 1)

            def centre2(n):
                pe.wait_ge(h2_ready, n + 1)
                if exists(n + 2):
                    pe.wait_ge(h_ready, n + 3)
                mm(M0[:, 0:2 * W], center_sb[:, :], h2[:, :, :], start=True, stop=True).then_inc(xc2_done, 1)

            def variance2(n):
                pe.wait_ge(sq2_ready, n + 1)
                mm(M3[:, 0:2 * W], mean_sb[:, :], sq2[:, :], start=True, stop=True).then_inc(var2_done, 1)

            def ffn1(n):
                pe.wait_ge(xhat2_ready, n + 1)
                if exists(n + 2):
                    pe.wait_ge(std1_ready, n + 3)
                mm(M2[:, 0:2 * W], w1_sb[:, :], xhat2[:, :], start=True, stop=True).then_inc(ffn1_done, 1)

            def ffn2(n):
                pe.wait_ge(gelu_ready, n + 1)
                if exists(n + 2):
                    pe.wait_ge(q_hl_ready, 2 * n + 5)
                for m in range(2):
                    for tt, (t0, rows) in enumerate(TILE):
                        rows = KEYS[tt]
                        c = (2 * m + tt) * D
                        mm(M3[0:rows, c:c + D], h2[:, m, t0:t0 + rows], ident_sb[:, :], start=True, stop=False)
                        last = mm(M3[0:rows, c:c + D], gelu[:, m, t0:t0 + rows], w2_sb[:, :], start=False, stop=True)
                last.then_inc(ffn2_done, 1)

            def pair(n, half, par):
                prev, nxt = exists(n - 1), exists(n + 1)
                half_next = half if par == 0 else half + 1
                for u in range(8):
                    scores(n, par, 0, u)
                    if prev:
                        scores_t(n - 1, 1 - par, 1, u)
                    if nxt and u < STEPS:
                        embed(n + 1, half_next, 1 - par, u)
                if prev:
                    weigh_v(n - 1, 1 - par, 1)
                transpose_max(n, 0)
                for u in range(8):
                    scores(n, par, 1, u)
                    scores_t(n, par, 0, u)
                    if u == 0 and prev:
                        project_out(n - 1)
                    if u == 1 and nxt:
                        centre1(n + 1, 1 - par)
                    if u == 2 and prev:
                        centre2(n - 1)
                    if u == 3 and nxt:
                        variance1(n + 1)
                    if u == 4 and prev:
                        variance2(n - 1)
                    if u == 5 and nxt:
                        project_q(n + 1, 0)
                    if u == 6 and prev:
                        ffn1(n - 1)
                    if u == 6 and nxt:
                        project_q(n + 1, 1)
                    if u == 7 and nxt:
                        project_k(n + 1, 0)
                if nxt:
                    project_k(n + 1, 1)
                    project_v(n + 1)
                weigh_v(n, par, 0)
                if prev:
                    ffn2(n - 1)
                transpose_max(n, 1)

            pe.wait_ge(setup, SETUP)
            for t in range(STEPS):
                embed(0, 0, 0, t)
            centre1(0, 0)
            variance1(0)
            for g in range(G):
                project_q(0, g)
            for g in range(G):
                project_k(0, g)
            project_v(0)
            over_pairs(pe, pair, PAIRS - 1)
            n = PAIRS - 1
            for u in range(8):
                scores_t(n, n % 2, 1, u)
            weigh_v(n, n % 2, 1)
            project_out(n)
            centre2(n)
            variance2(n)
            ffn1(n)
            ffn2(n)


def _layout(a):
    import numpy as np
    f = np.float32
    c = np.ascontiguousarray
    tok_w = np.asarray(a["L0_tok_W"]).reshape(D, C, PATCH, PATCH)
    wtok = np.zeros((SHIFTS, C, PATCH, STEPS, D), f)
    for s in range(SHIFTS):
        for t in range(STEPS):
            if SHIFTS * t + s < PATCH:
                wtok[s, :, :, t, :] = tok_w[:, :, :, SHIFTS * t + s].transpose(1, 2, 0)

    def twice(w):
        w = np.asarray(w).reshape(G, Q4, D, DK).transpose(2, 0, 1, 3)
        return c(np.stack([w, w], axis=3).reshape(D, G, 128))

    def twice_bias(b):
        b = np.asarray(b).reshape(G, Q4, DK)
        return np.stack([b, b], axis=2).reshape(G, 128).transpose(1, 0)

    wo = np.zeros((Q4, 32, G, D), f)
    wo[:, 0:DK, :, :] = np.asarray(a["L0_attn_out_w"]).reshape(D, DK, G, Q4).transpose(3, 1, 2, 0)
    cols = np.zeros((128, 10), f)
    cols[:, 0] = np.asarray(a["L0_tok_b"])
    cols[:, 1] = np.asarray(a["L0_ffn_b1"])
    low = np.zeros((Q4, 32), f)
    low[:, 0:DK] = 1
    high = np.zeros((Q4, 32), f)
    high[:, DK:] = 1
    one = np.zeros((Q4, 32), f)
    one[:, DK] = 1
    cols[:, 2], cols[:, 3], cols[:, 4] = low.reshape(128), high.reshape(128), one.reshape(128)
    cols[:, 5:7] = twice_bias(a["L0_attn_q_bias"])
    cols[:, 7:9] = twice_bias(a["L0_attn_k_bias"])
    cols[:, 9] = EPS
    pos = np.asarray(a["L0_tok_pos"])
    pos_t = pos[1:].transpose(1, 0)
    mean = np.full((D, D), 1.0 / D, f)
    return dict(
        x=np.asarray(a["x"]), wtok=wtok.reshape(SHIFTS * ROWS, STEPS, D),
        wq=twice(a["L0_attn_q_proj"]), wk=twice(a["L0_attn_k_proj"]),
        wv=c(np.asarray(a["L0_attn_v_proj"]).transpose(1, 0, 2).reshape(D, D)),
        wo=wo.reshape(128, G, D),
        w1=c(np.asarray(a["L0_ffn_W1"]).transpose(1, 0)), w2=c(np.asarray(a["L0_ffn_W2"]).transpose(1, 0)),
        tril_mask=np.triu(np.ones((D, D), f)), center=np.eye(D, dtype=f) - mean, mean=mean,
        ident=np.eye(D, dtype=f), pos2=c(np.stack([pos_t, pos_t], axis=1)),
        cls_tok=c(np.asarray(a["L0_tok_token"]).reshape(D, 1)), cls_pos=c(pos[0].reshape(D, 1)), cols=cols,
        vbias=c(np.broadcast_to(np.asarray(a["L0_attn_v_bias"]).reshape(1, 1, D), (100, 2, D)).reshape(100, 2 * D)),
        b2=c(np.broadcast_to(np.asarray(a["L0_ffn_b2"]).reshape(1, 1, D), (100, 4, D)).reshape(100, 4 * D)),
    )


def kernel(**inputs):
    import numpy as _np
    import concourse.bacc as _bacc
    from concourse import mybir as _mybir
    from concourse.bass_utils import run_bass_kernel_spmd as _run

    nc = _bacc.Bacc("TRN2", target_bir_lowering=False, num_devices=1)
    arrays, args = {}, {}
    for name, a in _layout(inputs).items():
        a = _np.ascontiguousarray(a)
        arrays[f"in_{name}"] = a
        args[name] = nc.dram_tensor(f"in_{name}", a.shape, _mybir.dt.from_np(a.dtype), kind="ExternalInput").ap()
    out = nc.dram_tensor("out_0", (B, SEQ, D), F32, kind="ExternalOutput").ap()
    vit_kernel(nc, out=out, **args)
    r = _run(nc, [arrays], core_ids=[0])
    return r.results[0]["out_0"]
```

```python
import concourse.bass as bass
from concourse import mybir
from contextlib import ExitStack

F32 = mybir.dt.float32
F32R = mybir.dt.float32r
ALU = mybir.AluOpType
ACT = mybir.ActivationFunctionType
AX = mybir.AxisListType

B, C, IMG, GRID, D, H, DK = 128, 3, 196, 14, 128, 8, 16
PATCH = IMG // GRID
NPATCH = GRID * GRID
SEQ = NPATCH + 1
W = SEQ + 1
PAIRS = B // 2
SHIFTS = 3
ROWS = C * PATCH
STEPS = -(-PATCH // SHIFTS)
XW = 2 * GRID * IMG
TILE = ((0, 100), (100, 98))
LAP = ((0, 100), (98, 100))
KEYS = (100, 97)
G = 2
Q4 = 4
EPS = 1e-5


def vit_kernel(nc, x, wtok, wq, wk, wv, wo, w1, w2, tril_mask, center, mean, ident, pos2, cls_tok, cls_pos,
               cols, vbias, b2, out):
    ctx = ExitStack()
    with ctx:
        def sb(name, shape, dt=F32):
            return ctx.enter_context(nc.sbuf_tensor(name, shape, dt))

        def sem(name):
            return ctx.enter_context(nc.semaphore(name))

        wtok_sb = sb("wtok_sb", [SHIFTS * ROWS, STEPS, D])
        wq_sb = sb("wq_sb", [D, G, 128])
        wk_sb = sb("wk_sb", [D, G, 128])
        wv_sb = sb("wv_sb", [D, D])
        wo_sb = sb("wo_sb", [D, D])
        w1_raw = sb("w1_raw", [D, D])
        w2_raw = sb("w2_raw", [D, D])
        w1_sb = sb("w1_sb", [D, D])
        w2_sb = sb("w2_sb", [D, D])
        tril_sb = sb("tril_sb", [D, D])
        center_sb = sb("center_sb", [D, D])
        mean_sb = sb("mean_sb", [D, D])
        ident_sb = sb("ident_sb", [D, D])
        neg_ident = sb("neg_ident", [D, 100], F32R)
        neg_half = sb("neg_half", [100, 4])
        pos_raw = sb("pos_raw", [D, 2, NPATCH])
        pos_b = sb("pos_b", [D, 2, NPATCH])
        cls_raw = sb("cls_raw", [D, 2])
        cols_sb = sb("cols_sb", [D, 10])
        vb_sb = sb("vb_sb", [100, 2 * D])
        b2_sb = sb("b2_sb", [100, 4 * D])
        tok_b, b1_c = cols_sb[:, 0:1], cols_sb[:, 1:2]
        eps_c = cols_sb[:, 9:10]
        mask_lo, mask_hi, one_16 = cols_sb[:, 2:3], cols_sb[:, 3:4], cols_sb[:, 4:5]
        qb = [cols_sb[:, 5 + g:6 + g] for g in range(G)]
        kb = [cols_sb[:, 7 + g:8 + g] for g in range(G)]
        qb_hi = sb("qb_hi", [D, G])

        pixels = [sb(f"pixels{p}", [SHIFTS * ROWS, XW]) for p in range(2)]
        h = [sb(f"h{p}", [D, 2, W]) for p in range(2)]
        h_kept = sb("h_kept", [D, 2, W])
        xc = [sb(f"xc{i}", [D, 2 * W]) for i in range(2)]
        sq = [sb(f"sq{i}", [D, 2 * W]) for i in range(2)]
        var = [sb(f"var{i}", [100, 4]) for i in range(2)]
        rstd = [sb(f"rstd{i}", [100, 4]) for i in range(2)]
        xhat = [sb(f"xhat{i}", [D, 2 * W]) for i in range(2)]
        q_sub = sb("q_sub", [128, G, 2, W], F32R)
        q_hl = [sb(f"q_hl{p}", [128, 2, G, W], F32R) for p in range(2)]
        k_hi = [sb(f"k_hi{p}", [128, 2, G, W], F32R) for p in range(2)]
        k_raw = sb("k_raw", [128, G, 2, W])
        k_lo = [sb(f"k_lo{p}", [128, 2, G, W], F32R) for p in range(2)]
        q_max = [sb(f"q_max{m}", [128, G * W], F32R) for m in range(2)]
        v = [sb(f"v{p}", [100, 2, 2, H, 32]) for p in range(2)]
        row_max = [sb(f"row_max{m}", [100, 2, G, 128], F32R) for m in range(2)]
        probs = [sb(f"probs{m}", [100, 2, Q4, G * W]) for m in range(2)]
        o_sb = sb("o_sb", [128, G * W])
        inv = sb("inv", [100, 2, G, Q4])
        o_tok = sb("o_tok", [100, 2, D])
        attn = sb("attn", [D, 2, W])
        pool_tick = sb("pool_tick", [128, 2])
        h2 = sb("h2", [D, 2, W])
        gelu = sb("gelu", [D, 2, W])
        out_sb = [sb(f"out_sb{p}", [100, 2, 2, D]) for p in range(2)]

        bank = [ctx.enter_context(nc.psum_tensor(f"bank{n}", [128, 512], F32)) for n in range(8)]
        M = bank[0:4]
        SA, ST = bank[4:6], bank[6:8]

        const_in = sem("const_in")
        pixels_in = [sem(f"pixels_in{p}") for p in range(2)]
        shifts_in = [sem(f"shifts_in{p}") for p in range(2)]
        stored = [sem(f"stored{p}") for p in range(2)]
        setup = sem("setup")
        ticked = sem("ticked")
        tok_done, xc_done = sem("tok_done"), [sem(f"xc_done{i}") for i in range(2)]
        var_done, spread_done = [[sem(f"{s}{i}") for i in range(2)] for s in ("var_done", "spread_done")]
        q_done, k_done, v_done = sem("q_done"), sem("k_done"), sem("v_done")
        score_done = sem("score_done")
        score_t_done = sem("score_t_done")
        max_t_done, pv_done = sem("max_t_done"), sem("pv_done")
        turn_done, unturn_done = sem("turn_done"), sem("unturn_done")
        oproj_done, ffn1_done, ffn2_done = sem("oproj_done"), sem("ffn1_done"), sem("ffn2_done")
        h_ready, h_kept_ready = sem("h_ready"), sem("h_kept_ready")
        sq_ready, var_ready, rstd_ready, xhat_ready = [
            [sem(f"{s}{i}") for i in range(2)] for s in ("sq_ready", "var_ready", "rstd_ready", "xhat_ready")]
        q_hl_ready, k_raw_ready, v_ready = sem("q_hl_ready"), sem("k_raw_ready"), sem("v_ready")
        max_ready = sem("max_ready")
        q_max_ready, attn_ready = sem("q_max_ready"), sem("attn_ready")
        o_ready = sem("o_ready")
        inv_ready, o_tok_ready = sem("inv_ready"), sem("o_tok_ready")
        h2_ready, out_ready, gelu_ready = sem("h2_ready"), sem("out_ready"), sem("gelu_ready")
        q_sub_ready, k_hi_ready = sem("q_sub_ready"), sem("k_hi_ready")
        exp_ready = sem("exp_ready")
        k_lo_ready = sem("k_lo_ready")

        def upto(eng, s, count):
            if not isinstance(count, int) or count > 0:
                eng.wait_ge(s, count)

        def exists(n):
            return not isinstance(n, int) or 0 <= n < PAIRS

        def over_pairs(eng, body):
            for n in range(2):
                body(n, 0, n)
            loops = (PAIRS - 4) // 2
            with eng.Fori(0, loops) as k:
                body(2 * k + 2, k + 1, 0)
                body(2 * k + 3, k + 1, 1)
            for n in range(2 * loops + 2, PAIRS + 2):
                body(n, n // 2, n % 2)

        consts = [(wtok_sb, wtok), (wq_sb, wq), (wk_sb, wk), (wv_sb, wv), (wo_sb, wo), (w1_raw, w1), (w2_raw, w2),
                  (tril_sb, tril_mask), (center_sb, center), (mean_sb, mean), (ident_sb, ident),
                  (pos_raw, pos2), (cols_sb, cols), (vb_sb, vbias), (b2_sb, b2)]
        CONSTS = 16 * (len(consts) + 2)
        SETUP = 13

        block = ctx.enter_context(nc.Block())

        @block.sync
        def _(sp):
            def load_pixels(n, half, par):
                if not isinstance(n, int) or n >= 2:
                    sp.wait_ge(tok_done, n - 1)
                for m in range(2):
                    for c in range(C):
                        sp.dma_start(
                            pixels[par][PATCH * c:PATCH * (c + 1), m * XW // 2:(m + 1) * XW // 2],
                            x[bass.ds(2 * n + m, 1), c, :, :].rearrange("m (i p) w -> p (m i) w", p=PATCH),
                        ).then_inc(pixels_in[par], 16)
                sp.wait_ge(pixels_in[par], 96 * (half + 1))
                for s in range(1, SHIFTS):
                    sp.dma_start(pixels[par][ROWS * s:ROWS * (s + 1), 0:XW - s],
                                 pixels[par][0:ROWS, s:XW]).then_inc(shifts_in[par], 16)

            def store(n, half, par):
                sp.wait_ge(out_ready, n + 1)
                tokens = out[bass.ds(2 * n, 2), :, :].rearrange("m t d -> t m d")
                for t0, rows, src in ((0, 100, out_sb[par][0:100, :, 0, :]),
                                      (100, 96, out_sb[par][0:96, :, 1, :]),
                                      (196, 1, out_sb[par][96:97, :, 1, :])):
                    sp.dma_start(tokens[t0:t0 + rows, :, :], src).then_inc(stored[par], 16)

            load_pixels(0, 0, 0)
            for dst, src in consts:
                sp.dma_start(dst[:], src).then_inc(const_in, 16)
            sp.dma_start(cls_raw[:, 0:1], cls_tok).then_inc(const_in, 16)
            sp.dma_start(cls_raw[:, 1:2], cls_pos).then_inc(const_in, 16)
            load_pixels(1, 0, 1)
            load_pixels(2, 1, 0)
            load_pixels(3, 1, 1)
            with sp.Fori(0, (PAIRS - 4) // 2) as k:
                load_pixels(2 * k + 4, k + 2, 0)
                store(2 * k, k, 0)
                load_pixels(2 * k + 5, k + 2, 1)
                store(2 * k + 1, k, 1)
            for n in range(PAIRS - 4, PAIRS):
                store(n, n // 2, n % 2)
            for p in range(2):
                sp.wait_ge(stored[p], 48 * PAIRS // 2)

        @block.gpsimd
        def _(pool):
            def carry_waits(tick):
                upto(pool, ticked, tick)
                nc.gpsimd.tensor_tensor(pool_tick[:, 1:2], pool_tick[:, 0:1], pool_tick[:, 0:1], ALU.add).then_inc(ticked, 1)

            def inverse_deviation(i, n):
                pool.wait_ge(var_ready[i], n + 1)
                nc.gpsimd.tensor_tensor(rstd[i][:, :], var[i][:, :], neg_half[:, :], ALU.pow).then_inc(rstd_ready[i], 1)

            def keep_h(n, par):
                pool.wait_ge(h_ready, n + 1)
                upto(pool, h2_ready, n)
                carry_waits(3 * n + 2)
                nc.gpsimd.tensor_copy(h_kept[:, :, :], h[par][:, :, :]).then_inc(h_kept_ready, 1)

            def low_part_of_k(n, par):
                for g in range(G):
                    pool.wait_ge(k_raw_ready, 2 * n + g + 1)
                    carry_waits(3 * n + g)
                    nc.gpsimd.tensor_scalar(k_lo[par][:, :, g, :], k_raw[:, g, :, :], mask_lo, one_16,
                                            ALU.mult, ALU.add).then_inc(k_lo_ready, 1)

            def pair(n, half, par):
                if exists(n + 1):
                    inverse_deviation(0, n + 1)
                if exists(n):
                    keep_h(n, par)
                if exists(n - 1):
                    inverse_deviation(1, n - 1)
                if exists(n + 1):
                    low_part_of_k(n + 1, 1 - par)

            pool.wait_ge(setup, SETUP)
            inverse_deviation(0, 0)
            low_part_of_k(0, 0)
            over_pairs(pool, pair)

        @block.scalar
        def _(act):
            def copy_and_square(i, n):
                act.wait_ge(xc_done[i], n + 1)
                upto(act, xhat_ready[i], n)
                nc.scalar.activation(xc[i][:, :], M[i][:, 0:2 * W], ACT.Copy)
                nc.scalar.activation(sq[i][:, :], M[i][:, 0:2 * W], ACT.Square).then_inc(sq_ready[i], 1)

            def variance(i, n):
                act.wait_ge(var_done[i], n + 1)
                nc.scalar.activation(var[i][:, :], M[i][0:100, 0:4], ACT.Identity, bias=eps_c[0:100, :])\
                    .then_inc(var_ready[i], 1)

            def q_high(n, g):
                act.wait_ge(q_done, 2 * n + g + 1)
                upto(act, q_hl_ready, 2 * n + g - 1)
                nc.scalar.activation(q_sub[:, g, :, :], M[2 + g][:, 0:2 * W], ACT.Identity,
                                     bias=qb_hi[:, g:g + 1], scale=mask_hi).then_inc(q_sub_ready, 1)

            def k_high(n, par, g):
                act.wait_ge(k_done, 2 * n + g + 1)
                nc.scalar.activation(k_hi[par][:, :, g, :], M[2 * g][:, 0:2 * W], ACT.Identity,
                                     bias=kb[g]).then_inc(k_hi_ready, 1)

            def exp(n, m, u):
                kt, j = divmod(u, Q4)
                act.wait_ge(score_t_done, 16 * n + 8 * m + u + 1)
                nc.scalar.activation(probs[m][0:KEYS[kt], kt, j, :], ST[u % 2][0:KEYS[kt], 0:G * W], ACT.Exp,
                                     scale=DK ** -0.5).then_inc(exp_ready, 1)

            def copy_o(n, m):
                act.wait_ge(pv_done, 2 * n + m + 1)
                upto(act, turn_done, 2 * n + m)
                nc.scalar.activation(o_sb[:, :], M[2][:, 0:G * W], ACT.Copy).then_inc(o_ready, 1)

            def keep_attn(n, m):
                act.wait_ge(unturn_done, 2 * n + m + 1)
                upto(act, oproj_done, n)
                nc.scalar.activation(attn[:, m, :], M[2][:, 0:W], ACT.Copy).then_inc(attn_ready, 1)

            def ffn_gelu(n):
                act.wait_ge(ffn1_done, n + 1)
                nc.scalar.activation(gelu[:, :, :], M[1][:, 0:2 * W], ACT.Gelu, bias=b1_c).then_inc(gelu_ready, 1)

            def pair(n, half, par):
                for s in range(8):
                    if exists(n - 1):
                        exp(n - 1, 1, s)
                    if s == 0 and exists(n - 1):
                        copy_o(n - 1, 0)
                    if s == 2 and exists(n - 1):
                        keep_attn(n - 1, 0)
                    if s == 3 and exists(n - 2):
                        ffn_gelu(n - 2)
                    if s == 7 and exists(n + 1):
                        copy_and_square(0, n + 1)
                for s in range(8, 16):
                    if exists(n):
                        exp(n, 0, s - 8)
                    if s == 8 and exists(n - 1):
                        copy_o(n - 1, 1)
                    if s == 9 and exists(n + 1):
                        variance(0, n + 1)
                    if s == 10 and exists(n - 1):
                        keep_attn(n - 1, 1)
                    if s == 12 and exists(n + 1):
                        q_high(n + 1, 0)
                    if s == 12 and exists(n - 1):
                        copy_and_square(1, n - 1)
                    if s == 13 and exists(n + 1):
                        q_high(n + 1, 1)
                    if s == 13 and exists(n - 1):
                        variance(1, n - 1)
                    if s == 14 and exists(n + 1):
                        k_high(n + 1, 1 - par, 0)
                        k_high(n + 1, 1 - par, 1)

            act.wait_ge(setup, SETUP)
            copy_and_square(0, 0)
            variance(0, 0)
            for g in range(G):
                q_high(0, g)
            for g in range(G):
                k_high(0, 0, g)
            over_pairs(act, pair)

        @block.vector
        def _(dve):
            def embed(n, par):
                dve.wait_ge(tok_done, n + 1)
                upto(dve, h_kept_ready, n - 1)
                nc.vector.tensor_tensor(h[par][:, :, 1:SEQ], M[0][:, 0:2 * NPATCH].rearrange("p (m t) -> p m t", m=2),
                                        pos_b[:, :, :], ALU.add).then_inc(h_ready, 1)

            def normalise(i, n):
                dve.wait_ge(spread_done[i], n + 1)
                nc.vector.tensor_tensor(xhat[i][:, :], xc[i][:, :], M[i][:, 0:2 * W], ALU.mult).then_inc(xhat_ready[i], 1)

            def q_split(n, par, g):
                dve.wait_ge(q_sub_ready, 2 * n + g + 1)
                upto(dve, q_max_ready, 2 * n - 2)
                nc.vector.scalar_tensor_tensor(
                    out=q_hl[par][:, :, g, :], in0=M[2 + g][:, 0:2 * W].rearrange("p (m t) -> p m t", m=2),
                    scalar=qb[g], in1=q_sub[:, g, :, :].bitcast(F32), op0=ALU.add, op1=ALU.subtract)\
                    .then_inc(q_hl_ready, 1)

            def k_split(n, par, g):
                dve.wait_ge(k_hi_ready, 2 * n + g + 1)
                upto(dve, k_lo_ready, 2 * n + g - 1)
                nc.vector.scalar_tensor_tensor(
                    out=k_raw[:, g, :, :], in0=M[2 * g][:, 0:2 * W].rearrange("p (m t) -> p m t", m=2),
                    scalar=kb[g], in1=k_hi[par][:, :, g, :].bitcast(F32), op0=ALU.add, op1=ALU.subtract)\
                    .then_inc(k_raw_ready, 1)

            def v_out(n, par):
                dve.wait_ge(v_done, n + 1)
                for kt, rows in enumerate((100, 98)):
                    last = nc.vector.tensor_tensor(
                        v[par][0:rows, :, kt, :, 0:DK],
                        M[3][0:rows, :].rearrange("p (m k h d) -> p m k h d", m=2, k=2, h=H)[:, :, kt, :, :],
                        vb_sb[0:rows, :].rearrange("p (m h d) -> p m h d", m=2, h=H), ALU.add)
                last.then_inc(v_ready, 1)

            def maximum(n, m, u):
                qt, j = divmod(u, Q4)
                rows = TILE[qt][1]
                dve.wait_ge(score_done, 16 * n + 8 * m + u + 1)
                if u == 0:
                    upto(dve, max_t_done, 2 * n + m - 1)
                nc.vector.reduce_max(row_max[m][0:rows, qt, :, 32 * j + DK:32 * j + DK + 1],
                                     SA[u % 2][0:rows, 0:G * W].rearrange("p (g t) -> p g t", g=G)[:, :, 0:SEQ],
                                     AX.X).then_inc(max_ready, 1)

            def add_max(n, par, m):
                dve.wait_ge(max_t_done, 2 * n + m + 1)
                nc.vector.scalar_tensor_tensor(
                    out=q_max[m][:, :], in0=q_hl[par][:, m, :, :].rearrange("p g t -> p (g t)").bitcast(F32),
                    scalar=mask_lo, in1=(M[3], M[0])[m][:, 0:G * W], op0=ALU.mult, op1=ALU.add)\
                    .then_inc(q_max_ready, 1)

            def divide(n, m):
                dve.wait_ge(turn_done, 2 * n + m + 1)
                turned = M[2][0:100, :].rearrange("p (t g j r) -> p t g j r", t=2, g=G, j=Q4)
                upto(dve, o_tok_ready, 2 * n + m)
                nc.vector.reciprocal(inv[:, :, :, :], turned[:, :, :, :, DK]).then_inc(inv_ready, 1)
                dve.wait_ge(inv_ready, 2 * n + m + 1)
                nc.vector.tensor_tensor(
                    o_tok[:, :, :].rearrange("p t (h d) -> p (t h) d", d=DK),
                    M[2][0:100, :].rearrange("p (a r) -> p a r", r=32)[:, :, 0:DK],
                    inv[:, :, :, :].rearrange("p t g j -> p (t g j)").unsqueeze(2).to_broadcast([100, 16, DK]),
                    ALU.mult).then_inc(o_tok_ready, 1)

            def residual(n):
                dve.wait_ge(oproj_done, n + 1)
                dve.wait_ge(h_kept_ready, n + 1)
                nc.vector.tensor_tensor(h2[:, :, :], M[1][:, 0:2 * W].rearrange("p (m t) -> p m t", m=2), h_kept[:, :, :],
                                        ALU.add).then_inc(h2_ready, 1)

            def output(n, half, par):
                dve.wait_ge(ffn2_done, n + 1)
                upto(dve, stored[par], 48 * half)
                for tt, rows in enumerate(KEYS):
                    last = nc.vector.tensor_tensor(
                        out_sb[par][0:rows, :, tt, :],
                        M[1][0:rows, :].rearrange("p (m t d) -> p m t d", m=2, t=2)[:, :, tt, :],
                        b2_sb[0:rows, 0:2 * D].rearrange("p (m d) -> p m d", m=2), ALU.add)
                last.then_inc(out_ready, 1)

            def pair(n, half, par):
                if exists(n - 1):
                    add_max(n - 1, 1 - par, 1)
                for s in range(8):
                    if exists(n):
                        maximum(n, 0, s)
                    if s == 1 and exists(n - 1):
                        divide(n - 1, 0)
                    if s == 5 and exists(n + 1):
                        embed(n + 1, 1 - par)
                    if s == 6 and exists(n - 2):
                        output(n - 2, half - 1, par)
                if exists(n):
                    add_max(n, par, 0)
                for s in range(8, 16):
                    if exists(n):
                        maximum(n, 1, s - 8)
                    if s == 9 and exists(n - 1):
                        divide(n - 1, 1)
                    if s == 11 and exists(n + 1):
                        normalise(0, n + 1)
                    if s == 11 and exists(n - 1):
                        residual(n - 1)
                    if s == 12 and exists(n + 1):
                        q_split(n + 1, 1 - par, 0)
                    if s == 13 and exists(n + 1):
                        q_split(n + 1, 1 - par, 1)
                    if s == 14 and exists(n + 1):
                        k_split(n + 1, 1 - par, 0)
                        k_split(n + 1, 1 - par, 1)
                    if s == 15 and exists(n + 1):
                        v_out(n + 1, 1 - par)
                    if s == 15 and exists(n - 1):
                        normalise(1, n - 1)

            nc.vector.memset(pool_tick[:, :], 0.0).then_inc(setup, 1)
            nc.vector.memset(neg_half[:, :], -0.5).then_inc(setup, 1)
            dve.wait_ge(const_in, CONSTS)
            nc.vector.tensor_tensor(w1_sb[:, :], w1_raw[:, :], tril_sb[:, :], ALU.mult).then_inc(setup, 1)
            nc.vector.tensor_tensor(w2_sb[:, :], w2_raw[:, :], tril_sb[:, :], ALU.mult).then_inc(setup, 1)
            nc.vector.tensor_scalar(neg_ident[:, :], ident_sb[:, 0:100], -1.0, None, ALU.mult).then_inc(setup, 1)
            nc.vector.tensor_scalar(pos_b[:, :, :], pos_raw[:, :, :], tok_b, None, ALU.add).then_inc(setup, 1)
            nc.vector.tensor_scalar(qb_hi[:, :], cols_sb[:, 5:7], mask_hi, None, ALU.mult).then_inc(setup, 1)
            for p in range(2):
                nc.vector.memset(h[p][:, :, W - 1:W], 0.0)
                for m in range(2):
                    last = nc.vector.tensor_tensor(h[p][:, m, 0:1], cls_raw[:, 0:1], cls_raw[:, 1:2], ALU.add)
                last.then_inc(setup, 1)
                nc.vector.memset(v[p][:, :, :, :, DK:32], 1.0).then_inc(setup, 1)
            for m in range(2):
                nc.vector.memset(row_max[m][:, :, :, :].bitcast(F32), 0.0).then_inc(setup, 1)
            dve.wait_ge(setup, SETUP)
            embed(0, 0)
            normalise(0, 0)
            for g in range(G):
                q_split(0, 0, g)
            for g in range(G):
                k_split(0, 0, g)
            v_out(0, 0)
            over_pairs(dve, pair)

        @block.tensor
        def _(pe):
            mm = nc.tensor.matmul

            def embed(n, half, par, t):
                rows = min(SHIFTS, PATCH - SHIFTS * t) * ROWS
                if t == 0:
                    pe.wait_ge(shifts_in[par], 32 * (half + 1))
                    if isinstance(n, int) and n == 1:
                        pe.wait_ge(k_raw_ready, 1)
                    else:
                        upto(pe, q_max_ready, 2 * n - 2)
                view = pixels[par][:, :].rearrange("p (r j q) -> p r j q", j=GRID, q=PATCH)
                last = mm(M[0][:, 0:2 * NPATCH], wtok_sb[0:rows, t, :], view[0:rows, :, :, SHIFTS * t],
                          start=t == 0, stop=t == STEPS - 1)
                if t == STEPS - 1:
                    last.then_inc(tok_done, 1)

            def centre(i, ready, tokens, n):
                pe.wait_ge(ready, n + 1)
                mm(M[i][:, 0:2 * W], center_sb[:, :], tokens[:, :, :], start=True, stop=True).then_inc(xc_done[i], 1)

            def variance(i, n):
                pe.wait_ge(sq_ready[i], n + 1)
                for m in range(2):
                    for tt, (t0, rows) in enumerate(LAP):
                        c = 2 * m + tt
                        last = mm(M[i][0:rows, c:c + 1], sq[i][:, m * W + t0:m * W + t0 + rows], mean_sb[:, 0:1],
                                  start=True, stop=True)
                last.then_inc(var_done[i], 1)

            def spread_deviation(i, n):
                pe.wait_ge(rstd_ready[i], n + 1)
                for m in range(2):
                    for tt, (t0, rows) in enumerate(LAP):
                        c = 2 * m + tt
                        last = mm(M[i][:, m * W + t0:m * W + t0 + rows], rstd[i][0:rows, c:c + 1].to_broadcast([rows, D]),
                                  ident_sb[0:rows, 0:rows], is_transpose=True, start=True, stop=True)
                last.then_inc(spread_done[i], 1)

            def project_q(n, g):
                pe.wait_ge(xhat_ready[0], n + 1)
                if g == 0:
                    upto(pe, attn_ready, 2 * n - 2)
                else:
                    upto(pe, q_max_ready, 2 * n - 1)
                mm(M[2 + g][:, 0:2 * W], wq_sb[:, g, :], xhat[0][:, :], start=True, stop=True).then_inc(q_done, 1)

            def project_k(n, g):
                if g == 1:
                    pe.wait_ge(q_hl_ready, 2 * n + 1)
                mm(M[2 * g][:, 0:2 * W], wk_sb[:, g, :], xhat[0][:, :], start=True, stop=True).then_inc(k_done, 1)

            def project_v(n):
                pe.wait_ge(q_hl_ready, 2 * n + 2)
                for m in range(2):
                    for kt, (t0, rows) in enumerate(TILE):
                        c = (2 * m + kt) * D
                        last = mm(M[3][0:rows, c:c + D], xhat[0][:, m * W + t0:m * W + t0 + rows], wv_sb[:, :],
                                  start=True, stop=True)
                last.then_inc(v_done, 1)

            def scores(n, par, m, u):
                unit = 16 * n + 8 * m + u
                qt, j = divmod(u, Q4)
                t0, rows = TILE[qt]
                r = slice(32 * j, 32 * j + 32)
                if m == 0 and u == 0:
                    pe.wait_ge(q_hl_ready, 2 * n + 2)
                    pe.wait_ge(k_hi_ready, 2 * n + 2)
                upto(pe, max_ready, unit - 1)
                for g in range(G):
                    last = mm(SA[u % 2][0:rows, g * W:(g + 1) * W], q_hl[par][r, m, g, t0:t0 + rows],
                              k_hi[par][r, m, g, :], start=True, stop=True)
                last.then_inc(score_done, 1)

            def transpose_max(n, m):
                pe.wait_ge(max_ready, 16 * n + 8 * m + 8)
                if m == 0:
                    pe.wait_ge(v_ready, n + 1)
                elif exists(n + 1):
                    pe.wait_ge(k_raw_ready, 2 * n + 3)
                for qt, (t0, rows) in enumerate(TILE):
                    for g in range(G):
                        last = mm((M[3], M[0])[m][:, g * W + t0:g * W + t0 + rows], row_max[m][0:rows, qt, g, :],
                                  neg_ident[0:rows, 0:rows], start=True, stop=True)
                last.then_inc(max_t_done, 1)

            def scores_t(n, par, m, u):
                unit = 16 * n + 8 * m + u
                kt, j = divmod(u, Q4)
                t0, rows = TILE[kt][0], KEYS[kt]
                r = slice(32 * j, 32 * j + 32)
                if u == 0:
                    pe.wait_ge(k_lo_ready, 2 * n + 2)
                    pe.wait_ge(q_max_ready, 2 * n + m + 1)
                upto(pe, exp_ready, unit - 1)
                for g in range(G):
                    c = slice(g * W, (g + 1) * W)
                    mm(ST[u % 2][0:rows, c], k_hi[par][r, m, g, t0:t0 + rows], q_hl[par][r, m, g, :],
                       start=True, stop=False)
                    last = mm(ST[u % 2][0:rows, c], k_lo[par][r, m, g, t0:t0 + rows], q_max[m][r, c],
                              start=False, stop=True)
                last.then_inc(score_t_done, 1)

            def weigh_v(n, par, m):
                pe.wait_ge(exp_ready, 16 * n + 8 * m + 8)
                if m == 1:
                    pe.wait_ge(attn_ready, 2 * n + 1)
                elif exists(n + 1):
                    pe.wait_ge(k_raw_ready, 2 * n + 4)
                for g in range(G):
                    for kt in range(2):
                        for j in range(Q4):
                            last = mm(M[2][32 * j:32 * j + 32, g * W:(g + 1) * W],
                                      v[par][0:KEYS[kt], m, kt, 4 * g + j, :],
                                      probs[m][0:KEYS[kt], kt, j, g * W:(g + 1) * W],
                                      start=kt == 0, stop=kt == 1)
                last.then_inc(pv_done, 1)

            def turn_output(n, m):
                pe.wait_ge(o_ready, 2 * n + m + 1)
                for g in range(G):
                    for tt, (t0, rows) in enumerate(LAP):
                        c = (G * tt + g) * 128
                        last = mm(M[2][0:rows, c:c + 128], o_sb[:, g * W + t0:g * W + t0 + rows], ident_sb[:, :],
                                  is_transpose=True, start=True, stop=True)
                last.then_inc(turn_done, 1)

            def turn_back(n, m):
                pe.wait_ge(o_tok_ready, 2 * n + m + 1)
                for tt, (t0, rows) in enumerate(LAP):
                    last = mm(M[2][:, t0:t0 + rows], o_tok[0:rows, tt, :], ident_sb[0:rows, 0:rows],
                              is_transpose=True, start=True, stop=True)
                last.then_inc(unturn_done, 1)

            def project_out(n):
                pe.wait_ge(attn_ready, 2 * n + 2)
                upto(pe, out_ready, n)
                last = mm(M[1][:, 0:2 * W], wo_sb[:, :], attn[:, :, :], start=True, stop=True)
                last.then_inc(oproj_done, 1)

            def ffn1(n):
                pe.wait_ge(xhat_ready[1], n + 1)
                mm(M[1][:, 0:2 * W], w1_sb[:, :], xhat[1][:, :], start=True, stop=True).then_inc(ffn1_done, 1)

            def ffn2(n, m):
                if m == 0:
                    pe.wait_ge(gelu_ready, n + 1)
                for tt, (t0, _) in enumerate(TILE):
                    rows = KEYS[tt]
                    dst = M[1][0:rows, (2 * m + tt) * D:(2 * m + tt + 1) * D]
                    mm(dst, h2[:, m, t0:t0 + rows], ident_sb[:, :], is_transpose=True, start=True, stop=False)
                    last = mm(dst, gelu[:, m, t0:t0 + rows], w2_sb[:, :], start=False, stop=True)
                if m == 1:
                    last.then_inc(ffn2_done, 1)

            def pair(n, half, par):
                half_next = half if par == 0 else half + 1
                if exists(n - 1):
                    transpose_max(n - 1, 1)
                for s in range(8):
                    if exists(n):
                        scores(n, par, 0, s)
                    if exists(n - 1):
                        scores_t(n - 1, 1 - par, 1, s)
                    if s == 0 and exists(n - 1):
                        weigh_v(n - 1, 1 - par, 0)
                    if s == 1 and exists(n - 1):
                        turn_output(n - 1, 0)
                    if s == 2 and exists(n - 1):
                        turn_back(n - 1, 0)
                    if 1 <= s <= STEPS and exists(n + 1):
                        embed(n + 1, half_next, 1 - par, s - 1)
                    if s == 3 and exists(n - 2):
                        ffn1(n - 2)
                    if s in (5, 6) and exists(n - 2):
                        ffn2(n - 2, s - 5)
                    if s == 7 and exists(n + 1):
                        centre(0, h_ready, h[1 - par], n + 1)
                if exists(n):
                    transpose_max(n, 0)
                for s in range(8, 16):
                    if exists(n):
                        scores(n, par, 1, s - 8)
                        scores_t(n, par, 0, s - 8)
                    if s == 8 and exists(n - 1):
                        weigh_v(n - 1, 1 - par, 1)
                    if s == 9 and exists(n - 1):
                        turn_output(n - 1, 1)
                    if s == 9 and exists(n + 1):
                        variance(0, n + 1)
                    if s == 10 and exists(n - 1):
                        turn_back(n - 1, 1)
                    if s == 11 and exists(n + 1):
                        spread_deviation(0, n + 1)
                    if s == 11 and exists(n - 1):
                        project_out(n - 1)
                    if s == 12 and exists(n + 1):
                        project_q(n + 1, 0)
                    if s == 12 and exists(n - 1):
                        centre(1, h2_ready, h2, n - 1)
                    if s == 13 and exists(n + 1):
                        project_q(n + 1, 1)
                    if s == 13 and exists(n - 1):
                        variance(1, n - 1)
                    if s == 14 and exists(n + 1):
                        project_k(n + 1, 0)
                        project_k(n + 1, 1)
                    if s == 15 and exists(n - 1):
                        spread_deviation(1, n - 1)
                    if s == 15 and exists(n + 1):
                        project_v(n + 1)

            pe.wait_ge(setup, SETUP)
            for t in range(STEPS):
                embed(0, 0, 0, t)
            centre(0, h_ready, h[0], 0)
            variance(0, 0)
            spread_deviation(0, 0)
            for g in range(G):
                project_q(0, g)
            for g in range(G):
                project_k(0, g)
            project_v(0)
            over_pairs(pe, pair)


def _layout(a):
    import numpy as np
    f = np.float32
    c = np.ascontiguousarray
    tok_w = np.asarray(a["L0_tok_W"]).reshape(D, C, PATCH, PATCH)
    wtok = np.zeros((SHIFTS, C, PATCH, STEPS, D), f)
    for s in range(SHIFTS):
        for t in range(STEPS):
            if SHIFTS * t + s < PATCH:
                wtok[s, :, :, t, :] = tok_w[:, :, :, SHIFTS * t + s].transpose(1, 2, 0)

    def twice(w):
        w = np.asarray(w).reshape(G, Q4, D, DK).transpose(2, 0, 1, 3)
        return c(np.stack([w, w], axis=3).reshape(D, G, 128))

    def twice_bias(b):
        b = np.asarray(b).reshape(G, Q4, DK)
        return np.stack([b, b], axis=2).reshape(G, 128).transpose(1, 0)

    wo = c(np.asarray(a["L0_attn_out_w"]).reshape(D, DK, H).transpose(2, 1, 0).reshape(D, D))
    cols = np.zeros((128, 10), f)
    cols[:, 0] = np.asarray(a["L0_tok_b"])
    cols[:, 1] = np.asarray(a["L0_ffn_b1"])
    low = np.zeros((Q4, 32), f)
    low[:, 0:DK] = 1
    high = np.zeros((Q4, 32), f)
    high[:, DK:] = 1
    one = np.zeros((Q4, 32), f)
    one[:, DK] = 1
    cols[:, 2], cols[:, 3], cols[:, 4] = low.reshape(128), high.reshape(128), one.reshape(128)
    cols[:, 5:7] = twice_bias(a["L0_attn_q_bias"])
    cols[:, 7:9] = twice_bias(a["L0_attn_k_bias"])
    cols[:, 9] = EPS
    pos = np.asarray(a["L0_tok_pos"])
    pos_t = pos[1:].transpose(1, 0)
    mean = np.full((D, D), 1.0 / D, f)
    return dict(
        x=np.asarray(a["x"]), wtok=wtok.reshape(SHIFTS * ROWS, STEPS, D),
        wq=twice(a["L0_attn_q_proj"]), wk=twice(a["L0_attn_k_proj"]),
        wv=c(np.asarray(a["L0_attn_v_proj"]).transpose(1, 0, 2).reshape(D, D)),
        wo=wo,
        w1=c(np.asarray(a["L0_ffn_W1"]).transpose(1, 0)), w2=c(np.asarray(a["L0_ffn_W2"]).transpose(1, 0)),
        tril_mask=np.triu(np.ones((D, D), f)), center=np.eye(D, dtype=f) - mean, mean=mean,
        ident=np.eye(D, dtype=f), pos2=c(np.stack([pos_t, pos_t], axis=1)),
        cls_tok=c(np.asarray(a["L0_tok_token"]).reshape(D, 1)), cls_pos=c(pos[0].reshape(D, 1)), cols=cols,
        vbias=c(np.broadcast_to(np.asarray(a["L0_attn_v_bias"]).reshape(1, 1, D), (100, 2, D)).reshape(100, 2 * D)),
        b2=c(np.broadcast_to(np.asarray(a["L0_ffn_b2"]).reshape(1, 1, D), (100, 4, D)).reshape(100, 4 * D)),
    )


def kernel(**inputs):
    import numpy as _np
    import concourse.bacc as _bacc
    from concourse import mybir as _mybir
    from concourse.bass_utils import run_bass_kernel_spmd as _run

    nc = _bacc.Bacc("TRN2", target_bir_lowering=False, num_devices=1)
    arrays, args = {}, {}
    for name, a in _layout(inputs).items():
        a = _np.ascontiguousarray(a)
        arrays[f"in_{name}"] = a
        args[name] = nc.dram_tensor(f"in_{name}", a.shape, _mybir.dt.from_np(a.dtype), kind="ExternalInput").ap()
    out = nc.dram_tensor("out_0", (B, SEQ, D), F32, kind="ExternalOutput").ap()
    vit_kernel(nc, out=out, **args)
    r = _run(nc, [arrays], core_ids=[0])
    return r.results[0]["out_0"]
```

```python
import concourse.bass as bass
from concourse import mybir
from contextlib import ExitStack

F32 = mybir.dt.float32
F32R = mybir.dt.float32r
ALU = mybir.AluOpType
ACT = mybir.ActivationFunctionType
AX = mybir.AxisListType

B, C, IMG, GRID, D, H, DK = 128, 3, 196, 14, 128, 8, 16
PATCH = IMG // GRID
NPATCH = GRID * GRID
SEQ = NPATCH + 1
W = SEQ + 1
PAIRS = B // 2
SHIFTS = 3
ROWS = C * PATCH
STEPS = -(-PATCH // SHIFTS)
XW = 2 * GRID * IMG
TILE = ((0, 100), (100, 98))
LAP = ((0, 100), (98, 100))
KEYS = (100, 97)
G = 2
Q4 = 4
EPS = 1e-5
UNITS_T = tuple(tuple(divmod(u, 8) for u in us) for us in (
    (6,), (7,), (8,), (9,), (10,), (11,), (12,), (13,), (), (14, 15), (16,), (17, 18), (), (19,), (20,), (21,)))


def vit_kernel(nc, x, wtok, wq, wk, wv, wo, w1, w2, tril_mask, ident, pos2, cls_tok, cls_pos,
               cols, vbias, b2, out):
    ctx = ExitStack()
    with ctx:
        def sb(name, shape, dt=F32):
            return ctx.enter_context(nc.sbuf_tensor(name, shape, dt))

        def sem(name):
            return ctx.enter_context(nc.semaphore(name))

        wtok_sb = sb("wtok_sb", [SHIFTS * ROWS, STEPS, D])
        wq_sb = sb("wq_sb", [D, G, 128])
        wk_sb = sb("wk_sb", [D, G, 128])
        wv_sb = sb("wv_sb", [D, D])
        wq_hl, wk_hl = [[sb(f"{w}_{part}", [D, G, 128], F32R) for part in ("hi", "lo")] for w in ("wq", "wk")]
        wo_sb = sb("wo_sb", [D, D])
        w1_raw = sb("w1_raw", [D, D])
        w2_raw = sb("w2_raw", [D, D])
        w1_sb = sb("w1_sb", [D, D])
        w2_sb = sb("w2_sb", [D, D])
        tril_sb = sb("tril_sb", [D, D])
        ident_sb = sb("ident_sb", [D, D])
        neg_ident = sb("neg_ident", [D, 100], F32R)
        neg_half = sb("neg_half", [100, 4])
        pos_raw = sb("pos_raw", [D, 2, NPATCH])
        pos_b = sb("pos_b", [D, 2, NPATCH])
        cls_raw = sb("cls_raw", [D, 2])
        cols_sb = sb("cols_sb", [D, 10])
        vb_sb = sb("vb_sb", [100, 2 * D])
        b2_sb = sb("b2_sb", [100, 4 * D])
        tok_b, b1_c = cols_sb[:, 0:1], cols_sb[:, 1:2]
        mask_lo, mask_hi = cols_sb[:, 2:3], cols_sb[:, 3:4]
        max_row = [cols_sb[:, c:c + 1] for c in (4, 9)]
        qb = [cols_sb[:, 5 + g:6 + g] for g in range(G)]
        kb = [cols_sb[:, 7 + g:8 + g] for g in range(G)]
        qb_hi = sb("qb_hi", [D, G])

        pixels = [sb(f"pixels{p}", [SHIFTS * ROWS, XW]) for p in range(2)]
        h = [sb(f"h{p}", [D, 2, W]) for p in range(2)]
        h_kept = sb("h_kept", [D, 2, W])
        stats = [sb(f"stats{i}", [100, 4, 6]) for i in range(2)]
        moments = [sb(f"moments{i}", [100, 4, 2]) for i in range(2)]
        var = [sb(f"var{i}", [100, 4]) for i in range(2)]
        rstd = [sb(f"rstd{i}", [100, 4]) for i in range(2)]
        x_tok = [sb(f"x_tok{i}", [100, 4, D]) for i in range(2)]
        xhat = [sb(f"xhat{i}", [D, 2 * W]) for i in range(2)]
        xhat_hl = [sb(f"xhat_{part}", [D, 2 * W], F32R) for part in ("hi", "lo")]
        q_sub = sb("q_sub", [128, G, 2, W], F32R)
        q_hl = [sb(f"q_hl{p}", [128, 2, G, W], F32R) for p in range(2)]
        k_hi = [sb(f"k_hi{p}", [128, 2, G, W], F32R) for p in range(2)]
        k_raw = sb("k_raw", [128, G, 2, W])
        k_lo = [sb(f"k_lo{p}", [128, 2, G, W], F32R) for p in range(2)]
        q_max = [sb(f"q_max{m}", [128, G * W], F32R) for m in range(2)]
        v = [sb(f"v{p}", [100, 2, 2, H, 32]) for p in range(2)]
        row_max = [sb(f"row_max{m}", [100, 2, 128], F32R) for m in range(2)]
        probs = [sb(f"probs{m}", [100, 2, Q4, G * W]) for m in range(2)]
        o_sb = sb("o_sb", [128, G * W])
        inv = sb("inv", [100, 2, G, Q4])
        o_tok = sb("o_tok", [100, 2, D])
        attn = sb("attn", [D, 2, W])
        pool_tick, dve_tick = sb("pool_tick", [128, 3]), sb("dve_tick", [128, 3])
        h2 = sb("h2", [D, 2, W])
        h2_tok = sb("h2_tok", [100, 4 * D])
        h2_b2 = sb("h2_b2", [100, 4 * D])
        gelu = sb("gelu", [D, 2, W])
        out_sb = [sb(f"out_sb{p}", [100, 2, 2, D]) for p in range(2)]

        bank = [ctx.enter_context(nc.psum_tensor(f"bank{n}", [128, 512], F32)) for n in range(8)]
        M = bank[0:4]
        SA, ST = bank[4:6], bank[6:8]
        Q_BANK, K_BANK = (M[1], M[3]), (M[0], M[1])

        const_in, wtok_in = sem("const_in"), sem("wtok_in")
        pixels_in = [sem(f"pixels_in{p}") for p in range(2)]
        shifts_in = [sem(f"shifts_in{p}") for p in range(2)]
        stored = [sem(f"stored{p}") for p in range(2)]
        setup, weight_split = sem("setup"), sem("weight_split")
        tok_done = sem("tok_done")
        turned_done, xhat_done = [[sem(f"{s}{i}") for i in range(2)] for s in ("turned_done", "xhat_done")]
        q_done, k_done, v_done = sem("q_done"), sem("k_done"), sem("v_done")
        score_done = sem("score_done")
        score_t_done = sem("score_t_done")
        max_t_done, pv_done = sem("max_t_done"), sem("pv_done")
        turn_done, unturn_done = sem("turn_done"), sem("unturn_done")
        oproj_done, ffn1_done, ffn2_done = sem("oproj_done"), sem("ffn1_done"), sem("ffn2_done")
        h_ready, h_kept_ready = sem("h_ready"), sem("h_kept_ready")
        stats_ready, moments_ready, var_ready, rstd_ready, x_tok_ready, xhat_ready = [
            [sem(f"{s}{i}") for i in range(2)]
            for s in ("stats_ready", "moments_ready", "var_ready", "rstd_ready", "x_tok_ready", "xhat_ready")]
        h2_tok_ready, h2_b2_ready = sem("h2_tok_ready"), sem("h2_b2_ready")
        xhat_hl_ready = sem("xhat_hl_ready")
        q_hl_ready, k_raw_ready, v_ready = sem("q_hl_ready"), sem("k_raw_ready"), sem("v_ready")
        max_ready = sem("max_ready")
        q_max_ready, attn_ready = sem("q_max_ready"), sem("attn_ready")
        o_ready = sem("o_ready")
        inv_ready, o_tok_ready = sem("inv_ready"), sem("o_tok_ready")
        h2_ready, out_ready, gelu_ready = sem("h2_ready"), sem("out_ready"), sem("gelu_ready")
        q_sub_ready, k_hi_ready = sem("q_sub_ready"), sem("k_hi_ready")
        exp_ready = sem("exp_ready")
        k_lo_ready = sem("k_lo_ready")

        def upto(eng, s, count):
            if not isinstance(count, int) or count > 0:
                eng.wait_ge(s, count)

        def transposed_units(n, s):
            return [(n, 0, u) if m == 2 else (n - 1, m, u) for m, u in UNITS_T[s]]

        def exists(n):
            return not isinstance(n, int) or 0 <= n < PAIRS

        def over_pairs(eng, body):
            for n in range(2):
                body(n, 0, n)
            loops = (PAIRS - 4) // 2
            with eng.Fori(0, loops) as k:
                body(2 * k + 2, k + 1, 0)
                body(2 * k + 3, k + 1, 1)
            for n in range(2 * loops + 2, PAIRS + 2):
                body(n, n // 2, n % 2)

        consts = [(wq_sb, wq), (wk_sb, wk), (wv_sb, wv), (wo_sb, wo), (w1_raw, w1), (w2_raw, w2),
                  (tril_sb, tril_mask), (ident_sb, ident),
                  (pos_raw, pos2), (cols_sb, cols), (vb_sb, vbias), (b2_sb, b2)]
        CONSTS = 16 * (len(consts) + 2)
        SETUP = 18

        block = ctx.enter_context(nc.Block())

        @block.sync
        def _(sp):
            def load_pixels(n, half, par):
                if not isinstance(n, int) or n >= 2:
                    sp.wait_ge(tok_done, n - 1)
                for m in range(2):
                    for c in range(C):
                        sp.dma_start(
                            pixels[par][PATCH * c:PATCH * (c + 1), m * XW // 2:(m + 1) * XW // 2],
                            x[bass.ds(2 * n + m, 1), c, :, :].rearrange("m (i p) w -> p (m i) w", p=PATCH),
                        ).then_inc(pixels_in[par], 16)
                sp.wait_ge(pixels_in[par], 96 * (half + 1))
                for s in range(1, SHIFTS):
                    sp.dma_start(pixels[par][ROWS * s:ROWS * (s + 1), 0:XW - s],
                                 pixels[par][0:ROWS, s:XW]).then_inc(shifts_in[par], 16)

            def store(n, half, par):
                sp.wait_ge(out_ready, n + 1)
                tokens = out[bass.ds(2 * n, 2), :, :].rearrange("m t d -> t m d")
                for t0, rows, src in ((0, 100, out_sb[par][0:100, :, 0, :]),
                                      (100, 96, out_sb[par][2:98, :, 1, :]),
                                      (196, 1, out_sb[par][98:99, :, 1, :])):
                    sp.dma_start(tokens[t0:t0 + rows, :, :], src).then_inc(stored[par], 16)

            load_pixels(0, 0, 0)
            load_pixels(1, 0, 1)
            load_pixels(2, 1, 0)
            load_pixels(3, 1, 1)
            with sp.Fori(0, (PAIRS - 4) // 2) as k:
                load_pixels(2 * k + 4, k + 2, 0)
                store(2 * k, k, 0)
                load_pixels(2 * k + 5, k + 2, 1)
                store(2 * k + 1, k, 1)
            for n in range(PAIRS - 4, PAIRS):
                store(n, n // 2, n % 2)
            for p in range(2):
                sp.wait_ge(stored[p], 48 * PAIRS // 2)

        @block.gpsimd
        def _(pool):
            def carry_waits(column, before, count):
                upto(pool, before, count)
                nc.gpsimd.tensor_tensor(pool_tick[:, column:column + 1], pool_tick[:, 0:1], pool_tick[:, 0:1], ALU.add)

            def inverse_deviation(i, n):
                pool.wait_ge(var_ready[i], n + 1)
                nc.gpsimd.tensor_tensor(rstd[i][:, :], var[i][:, :], neg_half[:, :], ALU.pow).then_inc(rstd_ready[i], 1)

            def add_b2(n):
                pool.wait_ge(h2_tok_ready, n + 1)
                upto(pool, out_ready, n)
                nc.gpsimd.tensor_tensor(h2_b2[:, :], h2_tok[:, :], b2_sb[:, :], ALU.add).then_inc(h2_b2_ready, 1)

            def keep_h(n, par):
                pool.wait_ge(h_ready, n + 1)
                upto(pool, h2_ready, n)
                carry_waits(1, h_kept_ready, n)
                nc.gpsimd.tensor_copy(h_kept[:, :, :], h[par][:, :, :]).then_inc(h_kept_ready, 1)

            def low_part_of_k(n, par):
                for g in range(G):
                    pool.wait_ge(k_raw_ready, 2 * n + g + 1)
                    carry_waits(2, k_lo_ready, 2 * n + g)
                    nc.gpsimd.tensor_scalar(k_lo[par][:, :, g, :], k_raw[:, g, :, :], mask_lo, max_row[g],
                                            ALU.mult, ALU.add).then_inc(k_lo_ready, 1)

            def pair(n, half, par):
                if exists(n - 1):
                    keep_h(n - 1, 1 - par)
                if exists(n - 2):
                    inverse_deviation(1, n - 2)
                    add_b2(n - 2)
                if exists(n + 1):
                    inverse_deviation(0, n + 1)
                    low_part_of_k(n + 1, 1 - par)

            pool.wait_ge(setup, SETUP)
            inverse_deviation(0, 0)
            low_part_of_k(0, 0)
            over_pairs(pool, pair)

        @block.scalar
        def _(act):
            def keep_h2_tok(n):
                act.wait_ge(stats_ready[1], n + 1)
                upto(act, h2_b2_ready, n)
                nc.scalar.activation(h2_tok[:, :], M[1][0:100, :], ACT.Copy).then_inc(h2_tok_ready, 1)

            def keep_xhat(n):
                act.wait_ge(xhat_done[1], n + 1)
                nc.scalar.activation(xhat[1][:, :], M[1][:, 0:2 * W], ACT.Copy).then_inc(xhat_ready[1], 1)

            def q_high(n, g):
                act.wait_ge(q_done, 2 * n + g + 1)
                upto(act, q_hl_ready, 2 * n + g - 1)
                nc.scalar.activation(q_sub[:, g, :, :], Q_BANK[g][:, 0:2 * W], ACT.Identity,
                                     bias=qb_hi[:, g:g + 1], scale=mask_hi).then_inc(q_sub_ready, 1)

            def k_high(n, par, g):
                act.wait_ge(k_done, 2 * n + g + 1)
                nc.scalar.activation(k_hi[par][:, :, g, :], K_BANK[g][:, 0:2 * W], ACT.Identity,
                                     bias=kb[g]).then_inc(k_hi_ready, 1)

            def exp(n, m, u):
                kt, j = divmod(u, Q4)
                act.wait_ge(score_t_done, 16 * n + 8 * m + u + 1)
                nc.scalar.activation(probs[m][0:KEYS[kt], kt, j, :], ST[u % 2][0:KEYS[kt], 0:G * W], ACT.Exp,
                                     scale=DK ** -0.5).then_inc(exp_ready, 1)

            def copy_o(n, m):
                act.wait_ge(pv_done, 2 * n + m + 1)
                upto(act, turn_done, 2 * n + m)
                nc.scalar.activation(o_sb[:, :], M[2][:, 0:G * W], ACT.Copy).then_inc(o_ready, 1)

            def keep_attn(n, m):
                act.wait_ge(unturn_done, 2 * n + m + 1)
                upto(act, oproj_done, n)
                nc.scalar.activation(attn[:, m, :], M[2][:, 0:W], ACT.Copy).then_inc(attn_ready, 1)

            def ffn_gelu(n):
                act.wait_ge(ffn1_done, n + 1)
                nc.scalar.activation(gelu[:, :, :], M[1][:, 0:2 * W], ACT.Gelu, bias=b1_c).then_inc(gelu_ready, 1)

            def pair(n, half, par):
                for s in range(16):
                    if s == 15 and exists(n - 1):
                        keep_attn(n - 1, 1)
                    if s == 7 and exists(n - 2):
                        ffn_gelu(n - 2)
                    if s == 7 and exists(n - 1):
                        copy_o(n - 1, 0)
                    for p, m, u in transposed_units(n, s):
                        if exists(p):
                            exp(p, m, u)
                    if s == 4 and exists(n - 2):
                        keep_xhat(n - 2)
                    if s == 11 and exists(n + 1):
                        q_high(n + 1, 0)
                    if s == 12 and exists(n + 1):
                        q_high(n + 1, 1)
                    if s == 12 and exists(n + 1):
                        k_high(n + 1, 1 - par, 0)
                    if s == 14 and exists(n + 1):
                        k_high(n + 1, 1 - par, 1)
                    if s == 11 and exists(n - 1):
                        copy_o(n - 1, 1)
                    if s == 9 and exists(n - 1):
                        keep_attn(n - 1, 0)
                    if s == 3 and exists(n - 2):
                        keep_h2_tok(n - 2)

            act.dma_start(wtok_sb[:], wtok).then_inc(wtok_in, 16)
            for dst, src in consts:
                act.dma_start(dst[:], src).then_inc(const_in, 16)
            act.dma_start(cls_raw[:, 0:1], cls_tok).then_inc(const_in, 16)
            act.dma_start(cls_raw[:, 1:2], cls_pos).then_inc(const_in, 16)
            act.wait_ge(setup, SETUP)
            for g in range(G):
                q_high(0, g)
            for g in range(G):
                k_high(0, 0, g)
            over_pairs(act, pair)

        @block.vector
        def _(dve):
            def embed(n, par):
                dve.wait_ge(tok_done, n + 1)
                upto(dve, h_kept_ready, n - 1)
                nc.vector.tensor_tensor(h[par][:, :, 1:SEQ], M[0][:, 0:2 * NPATCH].rearrange("p (m t) -> p m t", m=2),
                                        pos_b[:, :, :], ALU.add).then_inc(h_ready, 1)

            def statistics(i, n):
                dve.wait_ge(turned_done[i], n + 1)
                for c in range(4):
                    last = nc.vector.bn_stats(stats[i][:, c, :], M[i][0:100, c * D:(c + 1) * D])
                last.then_inc(stats_ready[i], 1)
                dve.wait_ge(stats_ready[i], n + 1)
                nc.vector.tensor_tensor(dve_tick[:, i + 1:i + 2], dve_tick[:, 0:1], dve_tick[:, 0:1], ALU.add)
                for c in range(4):
                    last = nc.vector.bn_aggr(moments[i][:, c, :], stats[i][:, c, :])
                last.then_inc(moments_ready[i], 1)
                dve.wait_ge(moments_ready[i], n + 1)
                nc.vector.tensor_scalar(var[i][:, :], moments[i][:, :, 1], EPS, None, ALU.add).then_inc(var_ready[i], 1)

            def normalise(i, n):
                dve.wait_ge(rstd_ready[i], n + 1)
                if i == 1:
                    dve.wait_ge(h2_tok_ready, n + 1)
                upto(dve, xhat_done[i], n)
                for c in range(4):
                    last = nc.vector.tensor_scalar(x_tok[i][:, c, :], M[i][0:100, c * D:(c + 1) * D],
                                                   moments[i][:, c, 0:1], rstd[i][:, c:c + 1], ALU.subtract, ALU.mult)
                last.then_inc(x_tok_ready[i], 1)

            def keep_xhat(n):
                dve.wait_ge(xhat_done[0], n + 1)
                nc.vector.tensor_copy(xhat[0][:, :], M[0][:, 0:2 * W]).then_inc(xhat_ready[0], 1)

            def split_xhat(n):
                dve.wait_ge(xhat_ready[0], n + 1)
                upto(dve, v_done, n)
                nc.vector.tensor_copy(xhat_hl[0][:, :], xhat[0][:, :]).then_inc(xhat_hl_ready, 1)
                dve.wait_ge(xhat_hl_ready, 2 * n + 1)
                nc.vector.tensor_tensor(xhat_hl[1][:, :], xhat[0][:, :], xhat_hl[0][:, :].bitcast(F32), ALU.subtract)\
                    .then_inc(xhat_hl_ready, 1)

            def q_split(n, par, g):
                dve.wait_ge(q_sub_ready, 2 * n + g + 1)
                upto(dve, q_max_ready, 2 * n - 2)
                nc.vector.scalar_tensor_tensor(
                    out=q_hl[par][:, :, g, :], in0=Q_BANK[g][:, 0:2 * W].rearrange("p (m t) -> p m t", m=2),
                    scalar=qb[g], in1=q_sub[:, g, :, :].bitcast(F32), op0=ALU.add, op1=ALU.subtract)\
                    .then_inc(q_hl_ready, 1)

            def k_split(n, par, g):
                dve.wait_ge(k_hi_ready, 2 * n + g + 1)
                upto(dve, k_lo_ready, 2 * n + g - 1)
                nc.vector.scalar_tensor_tensor(
                    out=k_raw[:, g, :, :], in0=K_BANK[g][:, 0:2 * W].rearrange("p (m t) -> p m t", m=2),
                    scalar=kb[g], in1=k_hi[par][:, :, g, :].bitcast(F32), op0=ALU.add, op1=ALU.subtract)\
                    .then_inc(k_raw_ready, 1)

            def v_out(n, par):
                dve.wait_ge(v_done, n + 1)
                for kt, rows in enumerate((100, 98)):
                    last = nc.vector.tensor_tensor(
                        v[par][0:rows, :, kt, :, 0:DK],
                        M[3][0:rows, :].rearrange("p (m k h d) -> p m k h d", m=2, k=2, h=H)[:, :, kt, :, :],
                        vb_sb[0:rows, :].rearrange("p (m h d) -> p m h d", m=2, h=H), ALU.add)
                last.then_inc(v_ready, 1)

            def maximum(n, m, u):
                qt, j = divmod(u, Q4)
                rows = TILE[qt][1]
                dve.wait_ge(score_done, 16 * n + 8 * m + u + 1)
                if u == 0:
                    upto(dve, max_t_done, 2 * n + m - 1)
                nc.vector.reduce_max(row_max[m][0:rows, qt, 32 * j + DK:32 * j + DK + G],
                                     SA[u % 2][0:rows, 0:G * W].rearrange("p (g t) -> p g t", g=G)[:, :, 0:SEQ],
                                     AX.X).then_inc(max_ready, 1)

            def add_max(n, par, m):
                dve.wait_ge(max_t_done, 2 * n + m + 1)
                nc.vector.scalar_tensor_tensor(
                    out=q_max[m][:, :].rearrange("p (g t) -> p g t", g=G), in0=q_hl[par][:, m, :, :].bitcast(F32),
                    scalar=mask_lo, in1=M[3][:, 0:W].unsqueeze(1).to_broadcast([128, G, W]), op0=ALU.mult, op1=ALU.add)\
                    .then_inc(q_max_ready, 1)

            def divide(n, m):
                dve.wait_ge(turn_done, 2 * n + m + 1)
                turned = M[2][0:100, :].rearrange("p (t g j r) -> p t g j r", t=2, g=G, j=Q4)
                upto(dve, o_tok_ready, 2 * n + m)
                nc.vector.reciprocal(inv[:, :, :, :], turned[:, :, :, :, DK]).then_inc(inv_ready, 1)
                dve.wait_ge(inv_ready, 2 * n + m + 1)
                nc.vector.tensor_tensor(
                    o_tok[:, :, :].rearrange("p t (h d) -> p (t h) d", d=DK),
                    M[2][0:100, :].rearrange("p (a r) -> p a r", r=32)[:, :, 0:DK],
                    inv[:, :, :, :].rearrange("p t g j -> p (t g j)").unsqueeze(2).to_broadcast([100, 16, DK]),
                    ALU.mult).then_inc(o_tok_ready, 1)

            def residual(n):
                dve.wait_ge(oproj_done, n + 1)
                dve.wait_ge(h_kept_ready, n + 1)
                nc.vector.tensor_tensor(h2[:, :, :], M[1][:, 0:2 * W].rearrange("p (m t) -> p m t", m=2), h_kept[:, :, :],
                                        ALU.add).then_inc(h2_ready, 1)

            def output(n, half, par):
                dve.wait_ge(ffn2_done, n + 1)
                upto(dve, stored[par], 48 * half)
                dve.wait_ge(h2_b2_ready, n + 1)
                last = nc.vector.tensor_tensor(out_sb[par][:, :, :, :].rearrange("p m t d -> p (m t d)"), M[1][0:100, :],
                                               h2_b2[:, :], ALU.add)
                last.then_inc(out_ready, 1)

            def pair(n, half, par):
                for s in range(16):
                    if s == 1 and exists(n - 1):
                        add_max(n - 1, 1 - par, 1)
                    if s == 9 and exists(n):
                        add_max(n, par, 0)
                    if exists(n):
                        maximum(n, s // 8, s % 8)
                    if s == 0 and exists(n - 2):
                        residual(n - 2)
                    if s == 2 and exists(n - 2):
                        statistics(1, n - 2)
                    if s == 3 and exists(n - 2):
                        normalise(1, n - 2)
                    if s == 12 and exists(n + 1):
                        q_split(n + 1, 1 - par, 1)
                    if s == 8 and exists(n + 1):
                        normalise(0, n + 1)
                    if s == 9 and exists(n - 2):
                        output(n - 2, half - 1, par)
                    if s == 13 and exists(n - 1):
                        divide(n - 1, 1)
                    if s == 4 and exists(n + 1):
                        embed(n + 1, 1 - par)
                    if s == 6 and exists(n + 1):
                        statistics(0, n + 1)
                    if s == 10 and exists(n + 1):
                        keep_xhat(n + 1)
                    if s == 10 and exists(n + 1):
                        split_xhat(n + 1)
                    if s == 11 and exists(n + 1):
                        q_split(n + 1, 1 - par, 0)
                    if s == 13 and exists(n + 1):
                        k_split(n + 1, 1 - par, 0)
                    if s == 14 and exists(n + 1):
                        k_split(n + 1, 1 - par, 1)
                    if s == 15 and exists(n + 1):
                        v_out(n + 1, 1 - par)
                    if s == 8 and exists(n - 1):
                        divide(n - 1, 0)

            nc.vector.memset(pool_tick[:, :], 0.0).then_inc(setup, 1)
            nc.vector.memset(dve_tick[:, :], 0.0).then_inc(setup, 1)
            nc.vector.memset(neg_half[:, :], -0.5).then_inc(setup, 1)
            for p in range(2):
                nc.vector.memset(h[p][:, :, W - 1:W], 0.0).then_inc(setup, 1)
                nc.vector.memset(v[p][:, :, :, :, DK:32], 1.0).then_inc(setup, 1)
            for m in range(2):
                nc.vector.memset(row_max[m][:, :, :].bitcast(F32), 0.0).then_inc(setup, 1)
            dve.wait_ge(const_in, CONSTS)
            nc.vector.tensor_scalar(pos_b[:, :, :], pos_raw[:, :, :], tok_b, None, ALU.add).then_inc(setup, 1)
            for p in range(2):
                for m in range(2):
                    last = nc.vector.tensor_tensor(h[p][:, m, 0:1], cls_raw[:, 0:1], cls_raw[:, 1:2], ALU.add)
                last.then_inc(setup, 1)
            for i, (w, parts) in enumerate(((wq_sb, wq_hl), (wk_sb, wk_hl))):
                nc.vector.tensor_copy(parts[0][:], w[:]).then_inc(weight_split, 1)
                dve.wait_ge(weight_split, i + 1)
                nc.vector.tensor_tensor(parts[1][:], w[:], parts[0][:].bitcast(F32), ALU.subtract).then_inc(setup, 1)
            nc.vector.tensor_tensor(w1_sb[:, :], w1_raw[:, :], tril_sb[:, :], ALU.mult).then_inc(setup, 1)
            nc.vector.tensor_tensor(w2_sb[:, :], w2_raw[:, :], tril_sb[:, :], ALU.mult).then_inc(setup, 1)
            nc.vector.tensor_scalar(neg_ident[:, :], ident_sb[:, 0:100], -1.0, None, ALU.mult).then_inc(setup, 1)
            nc.vector.tensor_scalar(qb_hi[:, :], cols_sb[:, 5:7], mask_hi, None, ALU.mult).then_inc(setup, 1)
            dve.wait_ge(setup, SETUP)
            embed(0, 0)
            statistics(0, 0)
            normalise(0, 0)
            keep_xhat(0)
            split_xhat(0)
            for g in range(G):
                q_split(0, 0, g)
            for g in range(G):
                k_split(0, 0, g)
            v_out(0, 0)
            over_pairs(dve, pair)

        @block.tensor
        def _(pe):
            mm = nc.tensor.matmul

            def embed(n, half, par, t):
                rows = min(SHIFTS, PATCH - SHIFTS * t) * ROWS
                if t == 0:
                    pe.wait_ge(shifts_in[par], 32 * (half + 1))
                    upto(pe, k_raw_ready, 2 * n - 1)
                view = pixels[par][:, :].rearrange("p (r j q) -> p r j q", j=GRID, q=PATCH)
                last = mm(M[0][:, 0:2 * NPATCH], wtok_sb[0:rows, t, :], view[0:rows, :, :, SHIFTS * t],
                          start=t == 0, stop=t == STEPS - 1)
                if t == STEPS - 1:
                    last.then_inc(tok_done, 1)

            def turn_tokens(i, ready, tokens, n):
                pe.wait_ge(ready, n + 1)
                for m in range(2):
                    for tt, (t0, rows) in enumerate(LAP):
                        c = (2 * m + tt) * D
                        last = mm(M[i][0:rows, c:c + D], tokens[:, m, t0:t0 + rows], ident_sb[:, :],
                                  is_transpose=True, start=True, stop=True)
                last.then_inc(turned_done[i], 1)

            def turn_xhat(i, n):
                pe.wait_ge(x_tok_ready[i], n + 1)
                for m in range(2):
                    for tt, (t0, rows) in enumerate(LAP):
                        last = mm(M[i][:, m * W + t0:m * W + t0 + rows], x_tok[i][0:rows, 2 * m + tt, :],
                                  ident_sb[0:rows, 0:rows], is_transpose=True, start=True, stop=True)
                last.then_inc(xhat_done[i], 1)

            THREE = ((0, 0), (1, 0), (0, 1))

            def project_q(n, g):
                pe.wait_ge(xhat_hl_ready, 2 * n + 2)
                if g == 0:
                    upto(pe, out_ready, n - 2)
                else:
                    upto(pe, q_max_ready, 2 * n - 1)
                for i, (a, b) in enumerate(THREE):
                    last = mm(Q_BANK[g][:, 0:2 * W], wq_hl[b][:, g, :], xhat_hl[a][:, :], start=i == 0, stop=i == 2)
                last.then_inc(q_done, 1)

            def project_k(n, g):
                if g == 1:
                    pe.wait_ge(q_hl_ready, 2 * n + 1)
                for i, (a, b) in enumerate(THREE):
                    last = mm(K_BANK[g][:, 0:2 * W], wk_hl[b][:, g, :], xhat_hl[a][:, :], start=i == 0, stop=i == 2)
                last.then_inc(k_done, 1)

            def project_v(n):
                pe.wait_ge(q_hl_ready, 2 * n + 2)
                for m in range(2):
                    for kt, (t0, rows) in enumerate(TILE):
                        c = (2 * m + kt) * D
                        last = mm(M[3][0:rows, c:c + D], xhat[0][:, m * W + t0:m * W + t0 + rows], wv_sb[:, :],
                                  start=True, stop=True)
                last.then_inc(v_done, 1)

            def scores(n, par, m, u):
                unit = 16 * n + 8 * m + u
                qt, j = divmod(u, Q4)
                t0, rows = TILE[qt]
                r = slice(32 * j, 32 * j + 32)
                if m == 0 and u == 0:
                    pe.wait_ge(q_hl_ready, 2 * n + 2)
                    pe.wait_ge(k_hi_ready, 2 * n + 2)
                upto(pe, max_ready, unit - 1)
                for g in range(G):
                    last = mm(SA[u % 2][0:rows, g * W:(g + 1) * W], q_hl[par][r, m, g, t0:t0 + rows],
                              k_hi[par][r, m, g, :], start=True, stop=True)
                last.then_inc(score_done, 1)

            def transpose_max(n, m):
                pe.wait_ge(max_ready, 16 * n + 8 * m + 8)
                if m == 0:
                    pe.wait_ge(v_ready, n + 1)
                elif exists(n + 1):
                    pe.wait_ge(v_ready, n + 2)
                for qt, (t0, rows) in enumerate(TILE):
                    last = mm(M[3][:, t0:t0 + rows], row_max[m][0:rows, qt, :], neg_ident[0:rows, 0:rows],
                              start=True, stop=True)
                last.then_inc(max_t_done, 1)

            def scores_t(n, par, m, u):
                unit = 16 * n + 8 * m + u
                kt, j = divmod(u, Q4)
                t0, rows = TILE[kt][0], KEYS[kt]
                r = slice(32 * j, 32 * j + 32)
                if u == 0:
                    pe.wait_ge(k_lo_ready, 2 * n + 2)
                    pe.wait_ge(q_max_ready, 2 * n + m + 1)
                upto(pe, exp_ready, unit - 1)
                for g in range(G):
                    c = slice(g * W, (g + 1) * W)
                    mm(ST[u % 2][0:rows, c], k_hi[par][r, m, g, t0:t0 + rows], q_hl[par][r, m, g, :],
                       start=True, stop=False)
                    last = mm(ST[u % 2][0:rows, c], k_lo[par][r, m, g, t0:t0 + rows], q_max[m][r, c],
                              start=False, stop=True)
                last.then_inc(score_t_done, 1)

            def weigh_v(n, par, m, g):
                if g == 0:
                    pe.wait_ge(exp_ready, 16 * n + 8 * m + 8)
                    upto(pe, attn_ready, 2 * n + m)
                for kt in range(2):
                    for j in range(Q4):
                        last = mm(M[2][32 * j:32 * j + 32, g * W:(g + 1) * W],
                                  v[par][0:KEYS[kt], m, kt, 4 * g + j, :],
                                  probs[m][0:KEYS[kt], kt, j, g * W:(g + 1) * W],
                                  start=kt == 0, stop=kt == 1)
                if g == 1:
                    last.then_inc(pv_done, 1)

            def turn_output(n, m):
                pe.wait_ge(o_ready, 2 * n + m + 1)
                for g in range(G):
                    for tt, (t0, rows) in enumerate(LAP):
                        c = (G * tt + g) * 128
                        last = mm(M[2][0:rows, c:c + 128], o_sb[:, g * W + t0:g * W + t0 + rows], ident_sb[:, :],
                                  is_transpose=True, start=True, stop=True)
                last.then_inc(turn_done, 1)

            def turn_back(n, m):
                pe.wait_ge(o_tok_ready, 2 * n + m + 1)
                for tt, (t0, rows) in enumerate(LAP):
                    last = mm(M[2][:, t0:t0 + rows], o_tok[0:rows, tt, :], ident_sb[0:rows, 0:rows],
                              is_transpose=True, start=True, stop=True)
                last.then_inc(unturn_done, 1)

            def project_out(n):
                pe.wait_ge(attn_ready, 2 * n + 2)
                if exists(n + 2):
                    pe.wait_ge(k_raw_ready, 2 * n + 6)
                else:
                    pe.wait_ge(out_ready, n)
                last = mm(M[1][:, 0:2 * W], wo_sb[:, :], attn[:, :, :], start=True, stop=True)
                last.then_inc(oproj_done, 1)

            def ffn1(n):
                pe.wait_ge(xhat_ready[1], n + 1)
                mm(M[1][:, 0:2 * W], w1_sb[:, :], xhat[1][:, :], start=True, stop=True).then_inc(ffn1_done, 1)

            def ffn2(n, m):
                if m == 0:
                    pe.wait_ge(gelu_ready, n + 1)
                for tt, (t0, rows) in enumerate(LAP):
                    last = mm(M[1][0:rows, (2 * m + tt) * D:(2 * m + tt + 1) * D], gelu[:, m, t0:t0 + rows], w2_sb[:, :],
                              start=True, stop=True)
                if m == 1:
                    last.then_inc(ffn2_done, 1)

            def pair(n, half, par):
                half_next = half if par == 0 else half + 1
                for s in range(16):
                    if exists(n):
                        scores(n, par, s // 8, s % 8)
                    if s == 1 and exists(n - 1):
                        transpose_max(n - 1, 1)
                    if s == 9 and exists(n):
                        transpose_max(n, 0)
                    for p, m, u in transposed_units(n, s):
                        if exists(p):
                            scores_t(p, par if p is n else 1 - par, m, u)
                    if s == 10 and exists(n + 1):
                        turn_xhat(0, n + 1)
                    if s == 13 and exists(n - 1):
                        turn_output(n - 1, 1)
                    if s == 5 and exists(n - 1):
                        weigh_v(n - 1, 1 - par, 0, 0)
                    if s == 7 and exists(n - 1):
                        weigh_v(n - 1, 1 - par, 0, 1)
                    if s == 10 and exists(n - 1):
                        weigh_v(n - 1, 1 - par, 1, 0)
                    if s == 10 and exists(n - 1):
                        weigh_v(n - 1, 1 - par, 1, 1)
                    if s == 0 and exists(n + 1):
                        embed(n + 1, half_next, 1 - par, 0)
                    if s == 1 and exists(n + 1):
                        embed(n + 1, half_next, 1 - par, 1)
                    if s == 2 and exists(n + 1):
                        embed(n + 1, half_next, 1 - par, 2)
                    if s == 4 and exists(n + 1):
                        embed(n + 1, half_next, 1 - par, 3)
                    if s == 4 and exists(n + 1):
                        embed(n + 1, half_next, 1 - par, 4)
                    if s == 6 and exists(n + 1):
                        turn_tokens(0, h_ready, h[1 - par], n + 1)
                    if s == 11 and exists(n + 1):
                        project_q(n + 1, 0)
                    if s == 15 and exists(n - 1):
                        turn_back(n - 1, 1)
                    if s == 12 and exists(n + 1):
                        project_q(n + 1, 1)
                    if s == 12 and exists(n + 1):
                        project_k(n + 1, 0)
                    if s == 14 and exists(n + 1):
                        project_k(n + 1, 1)
                    if s == 15 and exists(n + 1):
                        project_v(n + 1)
                    if s == 0 and exists(n - 2):
                        project_out(n - 2)
                    if s == 1 and exists(n - 2):
                        turn_tokens(1, h2_ready, h2, n - 2)
                    if s == 5 and exists(n - 2):
                        turn_xhat(1, n - 2)
                    if s == 6 and exists(n - 2):
                        ffn1(n - 2)
                    if s == 8 and exists(n - 2):
                        ffn2(n - 2, 0)
                    if s == 9 and exists(n - 2):
                        ffn2(n - 2, 1)
                    if s == 8 and exists(n - 1):
                        turn_output(n - 1, 0)
                    if s == 9 and exists(n - 1):
                        turn_back(n - 1, 0)

            pe.wait_ge(wtok_in, 16)
            for t in range(STEPS):
                embed(0, 0, 0, t)
            pe.wait_ge(setup, SETUP)
            turn_tokens(0, h_ready, h[0], 0)
            turn_xhat(0, 0)
            for g in range(G):
                project_q(0, g)
            for g in range(G):
                project_k(0, g)
            project_v(0)
            over_pairs(pe, pair)


def _layout(a):
    import numpy as np
    f = np.float32
    c = np.ascontiguousarray
    tok_w = np.asarray(a["L0_tok_W"]).reshape(D, C, PATCH, PATCH)
    wtok = np.zeros((SHIFTS, C, PATCH, STEPS, D), f)
    for s in range(SHIFTS):
        for t in range(STEPS):
            if SHIFTS * t + s < PATCH:
                wtok[s, :, :, t, :] = tok_w[:, :, :, SHIFTS * t + s].transpose(1, 2, 0)

    def twice(w):
        w = np.asarray(w).reshape(G, Q4, D, DK).transpose(2, 0, 1, 3)
        return c(np.stack([w, w], axis=3).reshape(D, G, 128))

    def twice_bias(b):
        b = np.asarray(b).reshape(G, Q4, DK)
        return np.stack([b, b], axis=2).reshape(G, 128).transpose(1, 0)

    wo = c(np.asarray(a["L0_attn_out_w"]).reshape(D, DK, H).transpose(2, 1, 0).reshape(D, D))
    cols = np.zeros((128, 10), f)
    cols[:, 0] = np.asarray(a["L0_tok_b"])
    cols[:, 1] = np.asarray(a["L0_ffn_b1"])
    low = np.zeros((Q4, 32), f)
    low[:, 0:DK] = 1
    high = np.zeros((Q4, 32), f)
    high[:, DK:] = 1
    one = np.zeros((G, Q4, 32), f)
    for g in range(G):
        one[g, :, DK + g] = 1
    cols[:, 2], cols[:, 3] = low.reshape(128), high.reshape(128)
    cols[:, 4], cols[:, 9] = one[0].reshape(128), one[1].reshape(128)
    cols[:, 5:7] = twice_bias(a["L0_attn_q_bias"])
    cols[:, 7:9] = twice_bias(a["L0_attn_k_bias"])
    pos = np.asarray(a["L0_tok_pos"])
    pos_t = pos[1:].transpose(1, 0)
    return dict(
        x=np.asarray(a["x"]), wtok=wtok.reshape(SHIFTS * ROWS, STEPS, D),
        wq=twice(a["L0_attn_q_proj"]), wk=twice(a["L0_attn_k_proj"]),
        wv=c(np.asarray(a["L0_attn_v_proj"]).transpose(1, 0, 2).reshape(D, D)),
        wo=wo,
        w1=c(np.asarray(a["L0_ffn_W1"]).transpose(1, 0)), w2=c(np.asarray(a["L0_ffn_W2"]).transpose(1, 0)),
        tril_mask=np.triu(np.ones((D, D), f)),
        ident=np.eye(D, dtype=f), pos2=c(np.stack([pos_t, pos_t], axis=1)),
        cls_tok=c(np.asarray(a["L0_tok_token"]).reshape(D, 1)), cls_pos=c(pos[0].reshape(D, 1)), cols=cols,
        vbias=c(np.broadcast_to(np.asarray(a["L0_attn_v_bias"]).reshape(1, 1, D), (100, 2, D)).reshape(100, 2 * D)),
        b2=c(np.broadcast_to(np.asarray(a["L0_ffn_b2"]).reshape(1, 1, D), (100, 4, D)).reshape(100, 4 * D)),
    )


def kernel(**inputs):
    import numpy as _np
    import concourse.bacc as _bacc
    from concourse import mybir as _mybir
    from concourse.bass_utils import run_bass_kernel_spmd as _run

    nc = _bacc.Bacc("TRN2", target_bir_lowering=False, num_devices=1)
    arrays, args = {}, {}
    for name, a in _layout(inputs).items():
        a = _np.ascontiguousarray(a)
        arrays[f"in_{name}"] = a
        args[name] = nc.dram_tensor(f"in_{name}", a.shape, _mybir.dt.from_np(a.dtype), kind="ExternalInput").ap()
    out = nc.dram_tensor("out_0", (B, SEQ, D), F32, kind="ExternalOutput").ap()
    vit_kernel(nc, out=out, **args)
    r = _run(nc, [arrays], core_ids=[0])
    return r.results[0]["out_0"]
```
